# Optimizing a Trainium2 kernel written in Bass

```python
import numpy as np
import jax
import jax.numpy as jnp

def _softmax(x, axis=-1):
    return jax.nn.softmax(x, axis=axis)

def _gelu(x):
    return jax.nn.gelu(x, approximate=True)

def _silu(x):
    return jax.nn.silu(x)

def _sigmoid(x):
    return jax.nn.sigmoid(x)

def _layernorm(x, axis=-1, eps=1e-05):
    m = jnp.mean(x, axis=axis, keepdims=True)
    v = jnp.var(x, axis=axis, keepdims=True)
    return (x - m) / jnp.sqrt(v + eps)

def _scatter_add(tgt, idx, src, axis=0):
    return tgt.at[idx].add(src)

def _segment_sum(src, seg, n):
    return jax.ops.segment_sum(src, seg, n)
kernel_name = 'mk_sandwich_d1_jaxref_r4_d6da75'

def setup_inputs(seed: int=0):
    np.random.seed(seed)
    _w = jnp.asarray

    def _L0_attn_setup():
        import jax, jax.numpy as jnp
        import numpy as np
        D_IN = 256
        D_OUT = 256
        NUM_HEADS = 16
        D_HEAD = D_OUT // NUM_HEADS
        key = jax.random.key(seed)
        ks = jax.random.split(key, 6)
        s = 0.02
        return {'x': jax.random.normal(ks[0], (2, 512, D_IN), dtype=jnp.float32), 'W_q': jax.random.normal(ks[1], (D_IN, D_OUT), dtype=jnp.float32) * s, 'W_k': jax.random.normal(ks[2], (D_IN, D_OUT), dtype=jnp.float32) * s, 'W_v': jax.random.normal(ks[3], (D_IN, D_OUT), dtype=jnp.float32) * s, 'W_o': jax.random.normal(ks[4], (D_OUT, D_OUT), dtype=jnp.float32) * s, 'b_o': jax.random.normal(ks[5], (D_OUT,), dtype=jnp.float32) * s}
    _L0_attn_in = _L0_attn_setup()

    def _L0_ffn_setup():
        import jax, jax.numpy as jnp
        import numpy as np
        N_EMBD = 256
        N_STATE = 1024
        key = jax.random.key(seed)
        k_x, k_w1, k_b1, k_w2, k_b2 = jax.random.split(key, 5)
        x = jax.random.normal(k_x, (4, 512, N_EMBD), dtype=jnp.float32)
        w1 = jax.random.normal(k_w1, (N_EMBD, N_STATE), dtype=jnp.float32) * (1.0 / np.sqrt(N_EMBD))
        b1 = jax.random.normal(k_b1, (N_STATE,), dtype=jnp.float32) * 0.02
        w2 = jax.random.normal(k_w2, (N_STATE, N_EMBD), dtype=jnp.float32) * (1.0 / np.sqrt(N_STATE))
        b2 = jax.random.normal(k_b2, (N_EMBD,), dtype=jnp.float32) * 0.02
        return {'x': x, 'w1': w1, 'b1': b1, 'w2': w2, 'b2': b2}
    _L0_ffn_in = _L0_ffn_setup()
    _d = {'L0_attn_x': _L0_attn_in['x'], 'L0_attn_W_q': _L0_attn_in['W_q'], 'L0_attn_W_k': _L0_attn_in['W_k'], 'L0_attn_W_v': _L0_attn_in['W_v'], 'L0_attn_W_o': _L0_attn_in['W_o'], 'L0_attn_b_o': _L0_attn_in['b_o'], 'L0_ffn_w1': _L0_ffn_in['w1'], 'L0_ffn_b1': _L0_ffn_in['b1'], 'L0_ffn_w2': _L0_ffn_in['w2'], 'L0_ffn_b2': _L0_ffn_in['b2']}
    _x0 = _d['L0_attn_x']
    _d['L0_attn_x'] = jax.random.normal(jax.random.fold_in(jax.random.key(seed), 1), (2, 2048, 256), dtype=_x0.dtype)
    del _x0
    return _d

def reference(L0_attn_x, L0_attn_W_q, L0_attn_W_k, L0_attn_W_v, L0_attn_W_o, L0_attn_b_o, L0_ffn_w1, L0_ffn_b1, L0_ffn_w2, L0_ffn_b2):

    def _L0_attn_ref(x, W_q, W_k, W_v, W_o, b_o):
        import jax, jax.numpy as jnp
        import numpy as np
        D_IN = 256
        D_OUT = 256
        NUM_HEADS = 16
        D_HEAD = D_OUT // NUM_HEADS
        B, T, _ = x.shape

        def split_heads(t):
            return t.reshape(B, T, NUM_HEADS, D_HEAD).transpose(0, 2, 1, 3)
        q = split_heads(x @ W_q)
        k = split_heads(x @ W_k)
        v = split_heads(x @ W_v)
        scores = jnp.einsum('bhqd,bhkd->bhqk', q, k)
        causal = jnp.triu(jnp.ones((T, T), dtype=bool), k=1)
        scores = jnp.where(causal, -jnp.inf, scores)
        attn = jax.nn.softmax(scores / np.sqrt(D_HEAD).astype(np.float32), axis=-1)
        ctx = jnp.einsum('bhqk,bhkd->bhqd', attn, v)
        ctx = ctx.transpose(0, 2, 1, 3).reshape(B, T, D_OUT)
        return ctx @ W_o + b_o

    def _L0_ffn_ref(x, w1, b1, w2, b2):
        import jax, jax.numpy as jnp
        import numpy as np
        N_EMBD = 256
        N_STATE = 1024
        h = jax.nn.gelu(jnp.einsum('bse,eh->bsh', x, w1) + b1, approximate=False)
        return jnp.einsum('bsh,he->bse', h, w2) + b2
    x = L0_attn_x
    x = x + _layernorm(_L0_attn_ref(_layernorm(x, axis=-1), L0_attn_W_q, L0_attn_W_k, L0_attn_W_v, L0_attn_W_o, L0_attn_b_o), axis=-1)
    x = x + _layernorm(_L0_ffn_ref(_layernorm(x, axis=-1), L0_ffn_w1, L0_ffn_b1, L0_ffn_w2, L0_ffn_b2), axis=-1)
    return x

_drawn_inputs = setup_inputs


def setup_inputs(seed=0):
    import zlib

    import numpy as np

    out = dict(_drawn_inputs(seed))
    spreads = {}
    factors = {'L0_ffn_b1': 4.66, 'L0_ffn_b2': 3.237}
    for name, (base, spread) in spreads.items():
        noise = np.random.default_rng([zlib.crc32(name.encode()), seed]).standard_normal(out[name].shape)
        drawn = base * np.exp(spread * noise) if base else spread * noise
        out[name] = jnp.asarray(drawn.astype(out[name].dtype))
    for name, factor in factors.items():
        out[name] = (out[name] * factor).astype(out[name].dtype)
    return out
```

```python
from contextlib import ExitStack

import concourse.bass as bass
from concourse import mybir

F32 = mybir.dt.float32
BF16 = mybir.dt.bfloat16
ALU = mybir.AluOpType
ACT = mybir.ActivationFunctionType
AX_X = mybir.AxisListType.X

P = 128
EPS = 1e-5
MASKED = -3.0e38


def at(n, per, plus=0):
    if isinstance(n, tuple):
        i, k = n
        return i * (2 * per) + (k * per + plus)
    return n * per + plus


def parity(n):
    return (n[1] if isinstance(n, tuple) else n) % 2


def nxt(n, k=1):
    return (n[0], n[1] + k) if isinstance(n, tuple) else n + k


def one(n):
    return bass.ds(at(n, 1), 1)


def attention_order(tiles_per_chunk, chunks, heads, with_max, pv_before):
    steps = [(c, j) for c in range(chunks) for j in range(tiles_per_chunk * (c + 1))]
    maxes = [(h, t, p) for h in range(heads) for t in range(tiles_per_chunk * chunks)
             for p in range(t // tiles_per_chunk + 1)]
    last = len(steps) - 1

    def cols(c, j):
        return tiles_per_chunk - max(0, j - tiles_per_chunk * c)

    def mcols(m):
        _, t, p = m
        return min(tiles_per_chunk, t + 1 - tiles_per_chunk * p)

    att_total = sum(cols(c, j) for c, j in steps[:last - 2])
    max_total = sum(mcols(m) for m in maxes)
    order, att, mx, m = [], 0, 0, 0

    def maxes_up_to(share, at_most):
        nonlocal mx, m
        while with_max and at_most > 0 and m < len(maxes) and mx < share * max_total:
            order.append(("max", m, *maxes[m]))
            mx += mcols(maxes[m])
            m += 1
            at_most -= 1

    for s, (c, j) in enumerate(steps):
        share = (att + cols(c, j)) / att_total
        order.append(("scores", s, c, j, 0))
        maxes_up_to(share, 1)
        order.append(("scores", s, c, j, 1))
        maxes_up_to(share, 1)
        if s > 0:
            order.append(("context", s - 1, *steps[s - 1]))
        elif pv_before:
            order.append(("context", -1, *steps[last]))
        maxes_up_to(share, 9)
        att += cols(c, j)
        if s == 1 and pv_before:
            order.append(("turn", -1))
        if s > 1 and steps[s - 2][0] != steps[s - 1][0]:
            order.append(("turn", c - 1))
        if with_max and m == len(maxes):
            order.append(("turn_max",))
            m += 1
    return order, steps, maxes


def sandwich_kernel(nc, x, w_q, w_k, w_v, w_o, b_o, w1, b1, w2, b2, out):
    B, T, C = x.shape
    HEADS, D = 16, C // 16
    S = w1.shape[1]
    CHUNK = 512
    TC = CHUNK // P
    NCH = B * T // CHUNK
    QC = T // CHUNK
    KT = T // P
    KC = C // P
    SM = S // P
    G = 4
    NG = B * HEADS // G
    GC = G * D
    PARTS = 3
    ROWS = 6 * D
    VW = 32
    PB = 4
    assert B == 2 and KC == 2 and QC == 4 and TC == 4

    x_v = x.rearrange("b (q t p) c -> p (b q) t c", t=TC, p=P)
    out_v = out.rearrange("b (q t p) c -> p (b q) t c", t=TC, p=P)
    parts_d = nc.dram_tensor("qk_parts", (2, PARTS, B, C, T), BF16, kind="Internal").ap()

    att, steps, maxes = {}, None, None
    for key in ((True, False), (True, True), (False, True)):
        att[key], steps, maxes = attention_order(TC, QC, G, *key)
    NS = len(steps)
    NM = len(maxes)
    ND = sum(j >= TC * c for c, j in steps)

    ctx = ExitStack()
    with ctx:
        def sb(name, shape, dt):
            return ctx.enter_context(nc.sbuf_tensor(name, shape, dt))

        def psum(name, shape, dt):
            return ctx.enter_context(nc.psum_tensor(name, shape, dt))

        def sem(name):
            return ctx.enter_context(nc.semaphore(name))

        score_ps = [psum(f"score_ps{h}", [P, 2, CHUNK], F32) for h in range(2)]
        ctx_ps = psum("ctx_ps", [P, CHUNK], F32)
        turn_ps = psum("turn_ps", [P, CHUNK], F32)
        max_ps = [psum(f"max_ps{m}", [P, CHUNK], F32) for m in range(2)]
        xt_ps = score_ps[0]
        qk_ps = [score_ps[1][:, 0, :], score_ps[1][:, 1, :], ctx_ps[:, :], turn_ps[:, :]]
        v_ps = max_ps
        y_ps = [score_ps[1][:, 0, :], score_ps[1][:, 1, :]]
        h_ps = [ctx_ps, turn_ps]
        f_ps = max_ps

        wq_sb = sb("wq_sb", [P, KC, C], F32)
        wk_sb = sb("wk_sb", [P, KC, C], F32)
        wv_sb = sb("wv_sb", [P, KC, C], F32)
        wo_sb = sb("wo_sb", [P, KC, C], F32)
        w1_sb = sb("w1_sb", [P, KC, S], F32)
        w2_sb = sb("w2_sb", [P, SM, C], F32)
        bo_sb = sb("bo_sb", [P, 2, C], F32)
        b2_sb = sb("b2_sb", [P, 2, C], F32)
        b1_sb = sb("b1_sb", [P, SM], F32)
        ident = sb("ident", [P, P], F32)
        ident_bf = sb("ident_bf", [P, P], BF16)
        causal = sb("causal", [P, CHUNK], F32)
        stats_sb = sb("stats", [P, 3, TC, 6], F32)
        meanvar_sb = sb("meanvar", [P, 3, TC, 2], F32)
        vareps = sb("vareps", [P, TC], F32)
        rstd = sb("rstd", [P, TC], F32)
        minus_half = sb("minus_half", [P, TC], F32)
        v_all = sb("v_all", [P, NCH, TC, C], F32)
        v_st = [sb(f"v_st{b}", [P, KT, G, VW], F32) for b in range(2)]
        probs = sb("probs", [P, PB, G, CHUNK], F32)
        max_junk = sb("max_junk", [P, 2, CHUNK], F32)
        max_parts = sb("max_parts", [P, G * KT, QC], F32)
        max_q = sb("max_q", [P, G * KT], F32)
        max_rest = sb("max_rest", [P, G * KT], F32)
        max_bf = sb("max_bf", [P, PARTS + 1, G * KT], BF16)
        max_rows = sb("max_rows", [P, 2, P], BF16)
        ctx_sb = [sb(f"ctx_sb{b}", [P, CHUNK], F32) for b in range(2)]
        rden = sb("rden", [P, TC, G], F32)
        arena = sb("arena", [P, 16384], F32)

        stacks = arena[:, :].bitcast(BF16).rearrange("p (b z g t) -> p b z g t", b=2, z=2, g=G)
        q_st = [stacks[:, b, 0] for b in range(2)]
        k_st = [stacks[:, b, 1] for b in range(2)]

        def carve(sizes, dt=F32):
            at_, views = carve.at, []
            for shape in sizes:
                size = 1
                for z in shape:
                    size *= z
                words = size if dt == F32 else size // 2
                v = arena[:, at_:at_ + words]
                if dt != F32:
                    v = v.bitcast(dt)
                if len(shape) == 2:
                    v = v.rearrange("p (a b) -> p a b", a=shape[0])
                views.append(v)
                at_ += words
            carve.at = at_
            assert at_ <= 16384
            return views

        carve.at = 0
        x_sb = carve([(TC, C)] * 2)
        xn_sb = carve([(TC, C)] * 2)
        xt_sb = carve([(KC, CHUNK)] * 2)
        rest_sb = carve([(CHUNK,)] * 4)
        part_sb = carve([(PARTS, CHUNK)] * 4, BF16)
        carve.at = 0
        res_sb = carve([(TC, C)] * 2)
        x1_sb = carve([(TC, C)] * 2)
        o_sb = carve([(TC, C)] * 2)
        cb_sb, = carve([(TC, C)])
        ct_sb, = carve([(KC, CHUNK)])
        yb_sb, = carve([(TC, C)])
        x1n_sb, = carve([(TC, C)])
        x1t_sb, = carve([(KC, CHUNK)])
        fb_sb, = carve([(TC, C)])
        ht_sb, = carve([(SM, CHUNK)])

        w_in = sem("w_in")
        consts = sem("consts")
        x_in = [sem(f"x_in{b}") for b in range(2)]
        ln_a = sem("ln_a")
        xn_ready = sem("xn_ready")
        xt_ready = sem("xt_ready")
        xt_copied = sem("xt_copied")
        qk_ready = sem("qk_ready")
        part1 = sem("part1")
        rest1 = sem("rest1")
        part2 = sem("part2")
        part3 = sem("part3")
        stored = [sem(f"stored{r}") for r in range(4)]
        v_ready = sem("v_ready")
        v_copied = sem("v_copied")
        phase_a = sem("phase_a")
        st_in = [[sem(f"st_in{b}{g}") for g in range(G)] for b in range(2)]
        mrow_in = [sem(f"mrow_in{b}") for b in range(2)]
        mx_ready = sem("mx_ready")
        mx_done = sem("mx_done")
        m_chain = sem("m_chain")
        mt_ready = sem("mt_ready")
        mt_copied = sem("mt_copied")
        sc_ready = sem("sc_ready")
        exp_done = sem("exp_done")
        masked = sem("masked")
        pv_done = sem("pv_done")
        vst_ready = sem("vst_ready")
        ctx_copied = sem("ctx_copied")
        turned = sem("turned")
        rden_done = sem("rden_done")
        ctx_done = sem("ctx_done")
        phase_b = sem("phase_b")
        res_in = [sem(f"res_in{b}") for b in range(2)]
        res_free = sem("res_free")
        cb_ready = sem("cb_ready")
        tp_ready = sem("tp_ready")
        tp_copied = sem("tp_copied")
        y_ready = sem("y_ready")
        y_taken = sem("y_taken")
        ln_y = sem("ln_y")
        x1_done = sem("x1_done")
        ln_x = sem("ln_x")
        x1n_ready = sem("x1n_ready")
        h_ready = sem("h_ready")
        gelu_done = sem("gelu_done")
        f_ready = sem("f_ready")
        f_taken = sem("f_taken")
        ln_f = sem("ln_f")
        o_ready = sem("o_ready")
        out_done = [sem(f"out_done{b}") for b in range(2)]
        dve_passed = sem("dve_passed")
        pool_passed = sem("pool_passed")
        N_WEIGHTS = 11

        block = ctx.enter_context(nc.Block())

        @block.sync
        def _(sp):
            for b in range(2):
                sp.dma_start(x_sb[b], x_v[:, b]).then_inc(x_in[b], 16)
            for w_sb, w in ((wq_sb, w_q), (wk_sb, w_k), (wv_sb, w_v), (wo_sb, w_o), (w1_sb, w1), (w2_sb, w2)):
                sp.dma_start(w_sb[:, :, :], w.rearrange("(k p) n -> p k n", p=P)).then_inc(w_in, 16)
            for b_sb, b in ((bo_sb, b_o), (b2_sb, b2)):
                for r in range(2):
                    sp.dma_start(b_sb[:, r, :], b.partition_broadcast(P)).then_inc(w_in, 16)
            with nc.allow_non_contiguous_dma(reason="1024 biases, once"):
                sp.dma_start(b1_sb[:, :], b1.rearrange("(m p) -> p m", p=P)).then_inc(w_in, 16)
            for r in range(4):
                sp.sem_inc(stored[r], 16)
            for b in range(2):
                sp.sem_inc(out_done[b], 16)

            def store_parts(n):
                for r in range(4):
                    sp.wait_ge(part3, at(n, 4, r + 1))
                    b, q = n // QC, n % QC
                    dst = parts_d[r // 2, :, b, (r % 2) * P:(r % 2 + 1) * P, q * CHUNK:(q + 1) * CHUNK]
                    sp.dma_start(dst.rearrange("s c t -> c s t"), part_sb[r]).then_inc(stored[r], 16)

            for n in range(NCH):
                store_parts(n)
                if n + 2 < NCH:
                    sp.wait_ge(xn_ready, n + 1)
                    sp.dma_start(x_sb[n % 2], x_v[:, n + 2]).then_inc(x_in[n % 2], 16)
            for r in range(4):
                sp.wait_ge(stored[r], 16 * (NCH + 1))
            sp.wait_ge(phase_a, 4)

            def load_stacks(n, hg, b):
                for g in range(G):
                    for st, qk, which in ((q_st, 0, (0, 0, 0, 1, 1, 2)), (k_st, 1, (0, 1, 2, 0, 1, 0))):
                        rows = parts_d[qk, :, b].rearrange("s (h e) t -> s h e t", e=D)
                        for r, part in enumerate(which):
                            src = rows[part, bass.ds(hg * G + g, 1)].rearrange("h e t -> (h e) t")
                            sp.dma_start(st[b][r * D:(r + 1) * D, g, :], src).then_inc(st_in[b][g], 16)

            def load_max_rows(n):
                sp.wait_ge(mt_copied, at(n, 1, 1))
                b = parity(n)
                for s in range(PARTS):
                    dst = q_st[b][ROWS + s:ROWS + s + 1].rearrange("o g (t q) -> o (g t) q", q=P)
                    src = max_rows[(s % 2) * G * KT:(s % 2 + 1) * G * KT, s // 2, :]
                    sp.dma_start(dst, src).then_inc(mrow_in[b], 16)

            load_stacks(0, 0, 0)
            load_stacks(1, 0, 1)
            load_max_rows(0)

            def slot(n, hg, last=False):
                load_max_rows(nxt(n))
                if not last:
                    sp.wait_ge(sc_ready, at(n, 2 * NS, 2 * NS))
                    load_stacks(nxt(n, 2), hg, parity(n))

            slot(0, 1)
            with sp.Fori(0, NG // 2 - 2) as i:
                slot((i, 1), i + 1)
                slot((i, 2), i + 2)
            slot(NG - 3, NG // 2 - 1)
            slot(NG - 2, 0, last=True)

            sp.wait_ge(phase_b, 4)
            for b in range(2):
                sp.dma_start(res_sb[b], x_v[:, b]).then_inc(res_in[b], 16)

            def store_out(n):
                sp.wait_ge(o_ready, at(n, 1, 1))
                b = parity(n)
                sp.dma_start(out_v[:, one(n)].rearrange("p o t c -> p (o t) c"), o_sb[b]).then_inc(out_done[b], 16)

            def load_res(n):
                sp.wait_ge(res_free, at(n, 1, -1))
                b = parity(n)
                sp.dma_start(res_sb[b], x_v[:, one(n)].rearrange("p o t c -> p (o t) c")).then_inc(res_in[b], 16)

            with sp.Fori(0, NCH // 2 - 1) as i:
                for k in range(2):
                    load_res((i, k + 2))
                    store_out((i, k))
            for n in (NCH - 2, NCH - 1):
                store_out(n)
            for b in range(2):
                sp.wait_ge(out_done[b], 16 * (NCH // 2 + 1))

        @block.gpsimd
        def _(pool):
            pool.memset(ident[:, :], 0.0)
            pool.memset(ident_bf[:, :], 0.0)
            pool.memset(minus_half[:, :], -0.5)
            pool.memset(causal[:, :], 0.0).then_inc(consts, 1)
            pool.wait_ge(consts, 1)
            pool.affine_select(ident[:, :], ident[:, :], [[-1, P]], ALU.not_equal, 1.0, 0, 1)
            pool.affine_select(ident_bf[:, :], ident_bf[:, :], [[-1, P]], ALU.not_equal, 1.0, 0, 1)
            pool.affine_select(causal[:, CHUNK - P:], causal[:, CHUNK - P:], [[-1, P]], ALU.is_ge,
                               MASKED, 0, 1).then_inc(consts, 1)
            for b in range(2):
                pool.memset(v_st[b][:, :, :, D:], 0.0)
            pool.memset(max_bf[:, PARTS, :], 0.0)
            pool.memset(max_parts[:, :, :], MASKED).then_inc(consts, 1)
            pool.wait_ge(consts, 3)
            pool.memset(v_st[0][:, :, :, D:D + 1], 1.0)
            pool.memset(v_st[1][:, :, :, D:D + 1], 1.0).then_inc(consts, 1)

            def inverse_root(chain, n, per):
                pool.wait_ge(chain, at(n, per, 3))
                pool.tensor_tensor(rstd[:, :], vareps[:, :], minus_half[:, :], ALU.pow).then_inc(chain, 1)

            with pool.Fori(0, NCH) as n:
                inverse_root(ln_a, n, 4)
            pool.drain().then_inc(phase_a, 1)

            pool.wait_ge(phase_a, 4)
            for b in range(2):
                pool.memset(k_st[b][ROWS:ROWS + PARTS, :, :], 1.0).then_inc(consts, 1)
                pool.wait_ge(consts, 5 + b)

            def stage_values(n, hg, b):
                v = v_all[:, b * QC:(b + 1) * QC, :, :].rearrange("p q t c -> p (q t) c")
                v = v[:, :, bass.ds(hg * GC, GC)].rearrange("p k (g e) -> p k g e", g=G)
                pool.tensor_copy(v_st[b][:, :, :, 0:D], v).then_inc(vst_ready, 1)

            def slot(n, key, hg):
                staged = not key[0]
                for e in att[key]:
                    if e[0] != "scores":
                        continue
                    _, s, c, j, h = e
                    if j < TC * c:
                        continue
                    off = (j - TC * c) * P
                    pool.wait_ge(exp_done, at(n, 2 * NS, 2 * s + h + 3))
                    pool.sem_inc(pool_passed, 1)
                    pr = probs[:, s % PB, 2 * h:2 * h + 2, off:off + P]
                    pool.affine_select(pr, pr, [[0, 2], [1, P]], ALU.is_ge, 0.0, 0, -1).then_inc(masked, 1)
                    if s == TC - 1 and h == 1 and not staged:
                        if n != 0:
                            pool.wait_ge(pv_done, at(n, NS, PB))
                        stage_values(nxt(n), hg, parity(nxt(n)))

            stage_values(0, 0, 0)
            slot(0, (True, False), 0)
            with pool.Fori(0, NG // 2 - 1) as i:
                slot((i, 1), (True, True), i + 1)
                slot((i, 2), (True, True), i + 1)
            slot(NG - 1, (False, True), 0)
            pool.drain().then_inc(phase_b, 1)
            pool.wait_ge(phase_b, 4)

            def fix_context(n):
                pool.wait_ge(tp_ready, at(n, 4, 2))
                pool.tensor_copy(cb_sb, v_all[:, one(n)].rearrange("p o t c -> p (o t) c")).then_inc(cb_ready, 1)

            def roots_before_mlp(n):
                inverse_root(ln_y, n, 5)
                inverse_root(ln_x, n, 4)

            fix_context(0)
            roots_before_mlp(0)
            fix_context(1)
            with pool.Fori(0, NCH // 2 - 1) as i:
                for k in range(2):
                    roots_before_mlp((i, k + 1))
                    fix_context((i, k + 2))
                    inverse_root(ln_f, (i, k), 5)
            roots_before_mlp(NCH - 1)
            inverse_root(ln_f, NCH - 2, 5)
            inverse_root(ln_f, NCH - 1, 5)

        @block.scalar
        def _(act):
            act.sem_inc(xt_copied, 2)
            act.sem_inc(v_copied, 2)
            act.sem_inc(exp_done, 2)
            act.sem_inc(ctx_copied, 1)
            act.sem_inc(tp_copied, 4)
            act.sem_inc(gelu_done, 2)

            def copy_xt(n):
                for k in range(KC):
                    act.wait_ge(xt_ready, at(n, 2, k + 5))
                    nc.scalar.copy(xt_sb[parity(n)][:, k, :], xt_ps[:, k, :]).then_inc(xt_copied, 1)

            def copy_v(n):
                for v in range(2):
                    act.wait_ge(v_ready, at(n, 2, v + 1))
                    dst = v_all[:, one(n), 2 * v:2 * v + 2, :].rearrange("p o t c -> p (o t c)")
                    nc.scalar.copy(dst, v_ps[v][:, :]).then_inc(v_copied, 1)

            def parts_12(n):
                def first(r):
                    act.wait_ge(qk_ready, at(n, 4, r + 1))
                    act.wait_ge(stored[r], at(n, 16, 16))
                    nc.scalar.copy(part_sb[r][:, 0, :], qk_ps[r]).then_inc(part1, 1)

                def second(r):
                    act.wait_ge(rest1, at(n, 4, r + 5))
                    nc.scalar.copy(part_sb[r][:, 1, :], rest_sb[r]).then_inc(part2, 1)

                first(0)
                for r in range(1, 4):
                    first(r)
                    second(r - 1)
                second(3)

            copy_xt(0)
            parts_12(0)
            with act.Fori(0, NCH // 2 - 1) as i:
                for k in (1, 2):
                    copy_xt((i, k))
                    copy_v((i, k - 1))
                    parts_12((i, k))
            copy_xt(NCH - 1)
            copy_v(NCH - 2)
            parts_12(NCH - 1)
            copy_v(NCH - 1)
            act.drain().then_inc(phase_a, 1)
            act.wait_ge(phase_a, 4)

            def copy_max_rows(n):
                act.wait_ge(mt_ready, at(n, 1, 1))
                src = turn_ps[:, 0:P].bitcast(BF16).rearrange("p (s q) -> p s q", s=2)
                nc.scalar.copy(max_rows[:, :, :], src).then_inc(mt_copied, 1)

            def copy_context(n, c):
                act.wait_ge(turned, at(n, QC, c + 1))
                nc.scalar.copy(ctx_sb[c % 2][:, :], ctx_ps[:, :]).then_inc(ctx_copied, 1)

            def slot(n, key):
                for e in att[key]:
                    if e[0] == "scores":
                        _, s, c, j, h = e
                        off = max(0, j - TC * c) * P
                        act.wait_ge(sc_ready, at(n, 2 * NS, 2 * s + h + 1))
                        act.wait_ge(pv_done, at(n, NS, s + 1))
                        nc.scalar.activation(probs[:, s % PB, 2 * h:2 * h + 2, off:], score_ps[h][:, :, off:],
                                             ACT.Exp, scale=1.0 / float(D) ** 0.5).then_inc(exp_done, 1)
                    elif e[0] == "context":
                        _, s, c, j = e
                        if j == TC * (c + 1) - 1:
                            act.wait_ge(pv_done, at(n, NS, s + 1 + PB))
                            if s < 0:
                                copy_context(nxt(n, -1), QC - 1)
                            else:
                                copy_context(n, c)
                    elif e[0] == "turn_max":
                        copy_max_rows(nxt(n))

            copy_max_rows(0)
            slot(0, (True, False))
            with act.Fori(0, NG // 2 - 1) as i:
                slot((i, 1), (True, True))
                slot((i, 2), (True, True))
            slot(NG - 1, (False, True))
            act.wait_ge(pv_done, NS * NG + PB)
            copy_context(NG - 1, QC - 1)
            act.drain().then_inc(phase_b, 1)
            act.wait_ge(phase_b, 4)
            act.wait_ge(w_in, 16 * N_WEIGHTS)

            def copy_turned(n, half, dst):
                for k in range(KC):
                    act.wait_ge(tp_ready, at(n, 4, 2 * half + k + 5))
                    if not half:
                        act.wait_ge(y_ready, at(n, 2, 2))
                    nc.scalar.copy(dst[:, k, :], xt_ps[:, k, :]).then_inc(tp_copied, 1)

            def gelu(n):
                act.wait_ge(f_ready, at(n, 2, 2))
                for m in range(SM):
                    act.wait_ge(h_ready, at(n, SM, m + 1))
                    nc.scalar.activation(ht_sb[:, m, :], h_ps[m % 2][:, :], ACT.Gelu,
                                         bias=b1_sb[:, m:m + 1]).then_inc(gelu_done, 1)

            copy_turned(0, 0, ct_sb)
            copy_turned(0, 1, x1t_sb)

            def chunk(n):
                copy_turned(nxt(n), 0, ct_sb)
                gelu(n)
                copy_turned(nxt(n), 1, x1t_sb)

            with act.Fori(0, NCH // 2 - 1) as i:
                chunk((i, 0))
                chunk((i, 1))
            chunk(NCH - 2)
            gelu(NCH - 1)

        @block.vector
        def _(dve):
            dve.sem_inc(rest1, 4)
            dve.sem_inc(mx_done, 2)
            dve.sem_inc(ctx_done, 1)
            dve.sem_inc(y_taken, 2)
            dve.sem_inc(f_taken, 2)

            def layer_norm(src, dst, chain, n, per, kind):
                stats, meanvar = stats_sb[:, kind], meanvar_sb[:, kind]
                for t in range(TC):
                    last = nc.vector.bn_stats(stats[:, t, :], src[:, t, :])
                last.then_inc(chain, 1)
                dve.wait_ge(chain, at(n, per, 1))
                dve.sem_inc(dve_passed, 1)
                for t in range(TC):
                    last = nc.vector.bn_aggr(meanvar[:, t, :], stats[:, t, :])
                last.then_inc(chain, 1)
                dve.wait_ge(chain, at(n, per, 2))
                nc.vector.tensor_scalar(vareps[:, :], meanvar[:, :, 1], EPS, None, ALU.add).then_inc(chain, 1)
                dve.wait_ge(chain, at(n, per, 4))
                for t in range(TC):
                    last = nc.vector.tensor_scalar(dst[:, t, :], src[:, t, :], meanvar[:, t, 0:1], rstd[:, t:t + 1],
                                                   ALU.subtract, ALU.mult)
                return last

            def norm_x(n):
                b = parity(n)
                dve.wait_ge(x_in[b], at(n, 8, 16 - 8 * b))
                dve.wait_ge(xt_ready, at(n, 2, 2))
                layer_norm(x_sb[b], xn_sb[b], ln_a, n, 4, b).then_inc(xn_ready, 1)

            def parts_3(n):
                def rest(r):
                    dve.wait_ge(part1, at(n, 4, r + 1))
                    nc.vector.tensor_tensor(rest_sb[r], qk_ps[r], part_sb[r][:, 0, :],
                                            ALU.subtract).then_inc(rest1, 1)

                def third(r):
                    dve.wait_ge(part2, at(n, 4, r + 1))
                    nc.vector.tensor_tensor(part_sb[r][:, 2, :], rest_sb[r], part_sb[r][:, 1, :],
                                            ALU.subtract).then_inc(part3, 1)

                rest(0)
                for r in range(1, 4):
                    rest(r)
                    third(r - 1)
                third(3)

            norm_x(0)
            norm_x(1)
            parts_3(0)
            with dve.Fori(0, NCH // 2 - 1) as i:
                for k in (1, 2):
                    norm_x((i, k + 1))
                    parts_3((i, k))
            parts_3(NCH - 1)
            dve.drain().then_inc(phase_a, 1)
            dve.wait_ge(phase_a, 4)

            def take_max(n, m, head, t, p):
                dve.wait_ge(mx_ready, at(n, NM, m + 1))
                w = min(TC, t + 1 - TC * p) * P
                dst = max_parts[:, head * KT + t, p:p + 1]
                src = max_ps[m % 2][:, 0:w]
                if p == t // TC:
                    dve.sem_inc(dve_passed, 1)
                    nc.vector.tensor_tensor_reduce(max_junk[:, m % 2, 0:w], src, causal[:, CHUNK - w:], 1.0, MASKED,
                                                   ALU.add, ALU.max, dst).then_inc(mx_done, 1)
                else:
                    nc.vector.reduce_max(dst, src, AX_X).then_inc(mx_done, 1)

            def split_max(n):
                dve.wait_ge(mx_done, at(n, NM, NM + 2))
                nc.vector.reduce_max(max_q[:, :], max_parts[:, :, :], AX_X).then_inc(m_chain, 1)
                dve.wait_ge(m_chain, at(n, 5, 1))
                nc.vector.tensor_scalar(max_bf[:, 0, :], max_q[:, :], -1.0, None, ALU.mult).then_inc(m_chain, 1)
                dve.wait_ge(m_chain, at(n, 5, 2))
                nc.vector.scalar_tensor_tensor(max_rest[:, :], max_q[:, :], -1.0, max_bf[:, 0, :],
                                               ALU.mult, ALU.subtract).then_inc(m_chain, 1)
                dve.wait_ge(m_chain, at(n, 5, 3))
                nc.vector.tensor_copy(max_bf[:, 1, :], max_rest[:, :]).then_inc(m_chain, 1)
                dve.wait_ge(m_chain, at(n, 5, 4))
                nc.vector.tensor_tensor(max_bf[:, 2, :], max_rest[:, :], max_bf[:, 1, :],
                                        ALU.subtract).then_inc(m_chain, 1)

            def normalise_context(n, c, hg, b):
                turn = turn_ps[:, :].rearrange("p (t g e) -> p t g e", t=TC, g=G)
                dve.wait_ge(turned, at(n, QC, c + 3))
                nc.vector.reciprocal(rden[:, :, :], turn[:, :, :, D]).then_inc(rden_done, 1)
                dve.wait_ge(rden_done, at(n, QC, c + 1))
                dst = v_all[:, b * QC + c, :, bass.ds(hg * GC, GC)].rearrange("p t (g e) -> p t g e", g=G)
                scale = rden[:, :, :].unsqueeze(3).to_broadcast([P, TC, G, D])
                nc.vector.tensor_tensor(dst, turn[:, :, :, 0:D], scale, ALU.mult).then_inc(ctx_done, 1)

            dve.wait_ge(consts, 3)
            for m in range(NM):
                take_max(0, m, *maxes[m])
            split_max(0)

            def slot(n, key, hg, hg_before):
                for e in att[key]:
                    if e[0] == "max":
                        take_max(nxt(n), *e[1:])
                    elif e[0] == "turn_max":
                        split_max(nxt(n))
                    elif e[0] == "turn":
                        if e[1] < 0:
                            normalise_context(nxt(n, -1), QC - 1, hg_before, parity(nxt(n, -1)))
                        else:
                            normalise_context(n, e[1], hg, parity(n))

            slot(0, (True, False), 0, 0)
            with dve.Fori(0, NG // 2 - 1) as i:
                slot((i, 1), (True, True), i, i)
                slot((i, 2), (True, True), i + 1, i)
            slot(NG - 1, (False, True), NG // 2 - 1, NG // 2 - 1)
            normalise_context(NG - 1, QC - 1, NG // 2 - 1, 1)
            dve.drain().then_inc(phase_b, 1)
            dve.wait_ge(phase_b, 4)
            dve.wait_ge(w_in, 16 * N_WEIGHTS)

            def attention_out(n):
                b = parity(n)
                for v in range(2):
                    dve.wait_ge(y_ready, at(n, 2, v + 3))
                    nc.vector.tensor_tensor(yb_sb[:, 2 * v:2 * v + 2, :],
                                            y_ps[v].rearrange("p (t c) -> p t c", t=2), bo_sb[:, :, :],
                                            ALU.add).then_inc(y_taken, 1)
                dve.wait_ge(y_taken, at(n, 2, 4))
                layer_norm(yb_sb, yb_sb, ln_y, n, 5, 0).then_inc(ln_y, 1)
                dve.wait_ge(ln_y, at(n, 5, 5))
                dve.wait_ge(res_in[b], at(n, 8, 16 - 8 * b))
                nc.vector.tensor_tensor(x1_sb[b], yb_sb, res_sb[b], ALU.add).then_inc(res_free, 1)
                dve.wait_ge(res_free, at(n, 1, 1))
                dve.wait_ge(tp_ready, at(n, 4, 4))
                layer_norm(x1_sb[b], x1n_sb, ln_x, n, 4, 1).then_inc(x1n_ready, 1)

            def mlp_out(n):
                b = parity(n)
                for v in range(2):
                    dve.wait_ge(f_ready, at(n, 2, v + 3))
                    nc.vector.tensor_tensor(fb_sb[:, 2 * v:2 * v + 2, :],
                                            f_ps[v][:, :].rearrange("p (t c) -> p t c", t=2), b2_sb[:, :, :],
                                            ALU.add).then_inc(f_taken, 1)
                dve.wait_ge(f_taken, at(n, 2, 4))
                layer_norm(fb_sb, fb_sb, ln_f, n, 5, 2).then_inc(ln_f, 1)
                dve.wait_ge(ln_f, at(n, 5, 5))
                dve.wait_ge(out_done[b], at(n, 8, 16 - 8 * b))
                nc.vector.tensor_tensor(o_sb[b], fb_sb, x1_sb[b], ALU.add).then_inc(o_ready, 1)

            attention_out(0)

            def chunk(n):
                attention_out(nxt(n))
                mlp_out(n)

            with dve.Fori(0, NCH // 2 - 1) as i:
                chunk((i, 0))
                chunk((i, 1))
            chunk(NCH - 2)
            dve.wait_ge(o_ready, NCH - 1)
            mlp_out(NCH - 1)

        @block.tensor
        def _(pe):
            pe.sem_inc(xt_ready, 4)
            pe.sem_inc(pv_done, PB)
            pe.sem_inc(turned, 2)
            pe.sem_inc(tp_ready, 4)
            pe.sem_inc(y_ready, 2)
            pe.sem_inc(f_ready, 2)
            pe.wait_ge(consts, 2)
            pe.wait_ge(w_in, 16 * N_WEIGHTS)

            def turn_x(n):
                pe.wait_ge(xn_ready, at(n, 1, 1))
                pe.wait_ge(xt_copied, at(n, 2, 2))
                for k in range(KC):
                    for t in range(TC):
                        last = nc.tensor.transpose(xt_ps[:, k, t * P:(t + 1) * P],
                                                   xn_sb[parity(n)][:, t, k * P:(k + 1) * P], ident[:, :])
                    last.then_inc(xt_ready, 1)

            def project_v(n):
                for v in range(2):
                    pe.wait_ge(v_copied, at(n, 2, v + 1))
                    for t in (2 * v, 2 * v + 1):
                        for k in range(KC):
                            last = nc.tensor.matmul(v_ps[v][:, (t % 2) * C:(t % 2 + 1) * C],
                                                    xt_sb[parity(n)][:, k, t * P:(t + 1) * P], wv_sb[:, k, :],
                                                    start=(k == 0), stop=(k == KC - 1))
                    last.then_inc(v_ready, 1)

            def project_qk(n):
                pe.wait_ge(xt_copied, at(n, 2, 4))
                for r in range(4):
                    w = (wq_sb, wk_sb)[r // 2]
                    pe.wait_ge(rest1, at(n, 4, r + 1))
                    for k in range(KC):
                        last = nc.tensor.matmul(qk_ps[r], w[:, k, (r % 2) * P:(r % 2 + 1) * P],
                                                xt_sb[parity(n)][:, k, :], start=(k == 0), stop=(k == KC - 1))
                    last.then_inc(qk_ready, 1)

            turn_x(0)
            project_qk(0)
            with pe.Fori(0, NCH // 2 - 1) as i:
                for k in (1, 2):
                    turn_x((i, k))
                    project_v((i, k - 1))
                    project_qk((i, k))
            turn_x(NCH - 1)
            project_v(NCH - 2)
            project_qk(NCH - 1)
            project_v(NCH - 1)
            pe.drain().then_inc(phase_a, 1)
            pe.wait_ge(phase_a, 4)
            pe.wait_ge(consts, 6)

            def max_scores(n, m, head, t, p):
                b = parity(n)
                if t == 0:
                    pe.wait_ge(st_in[b][head], at(n, 96, 192 - 96 * b))
                pe.wait_ge(mx_done, at(n, NM, m + 1))
                w = min(TC, t + 1 - TC * p) * P
                nc.tensor.matmul(max_ps[m % 2][:, 0:w], q_st[b][0:ROWS, head, t * P:(t + 1) * P],
                                 k_st[b][0:ROWS, head, p * CHUNK:p * CHUNK + w],
                                 start=True, stop=True).then_inc(mx_ready, 1)

            def turn_max(n):
                pe.wait_ge(m_chain, at(n, 5, 5))
                dst = turn_ps[:, 0:P].bitcast(BF16)
                for s in range(2):
                    last = nc.tensor.transpose(dst[:, s * P:(s + 1) * P],
                                               max_bf[:, 2 * s:2 * s + 2, :].rearrange("p s m -> p (s m)"),
                                               ident_bf[:, :])
                last.then_inc(mt_ready, 1)

            def scores(n, s, c, j, h):
                b = parity(n)
                off = max(0, j - TC * c) * P
                if s == 0 and h == 0:
                    pe.wait_ge(mrow_in[b], at(n, 24, 48 - 24 * b))
                pe.wait_ge(exp_done, at(n, 2 * NS, 2 * s + h + 1))
                for g in (0, 1):
                    last = nc.tensor.matmul(score_ps[h][:, g, off:],
                                            k_st[b][0:ROWS + PARTS, 2 * h + g, j * P:(j + 1) * P],
                                            q_st[b][0:ROWS + PARTS, 2 * h + g, c * CHUNK + off:(c + 1) * CHUNK],
                                            start=True, stop=True)
                last.then_inc(sc_ready, 1)

            def context(n, s, c, j):
                off = max(0, j - TC * c) * P
                if s == 0:
                    pe.wait_ge(vst_ready, at(n, 1, 1))
                if j == 0:
                    pe.wait_ge(ctx_copied, at(n, QC, c + 1))
                pe.wait_ge(exp_done, at(n, 2 * NS, 2 * s + 4))
                if j >= TC * c:
                    pe.wait_ge(masked, at(n, 2 * ND, 2 * (TC * c + j - TC * c) + 2))
                for g in range(G):
                    last = nc.tensor.matmul(ctx_ps[g * VW:(g + 1) * VW, off:], v_st[parity(n)][:, j, g, :],
                                            probs[:, s % PB, g, off:], start=(j == 0), stop=(j == TC * (c + 1) - 1))
                last.then_inc(pv_done, 1)

            def turn_context(n, c):
                pe.wait_ge(ctx_copied, at(n, QC, c + 2))
                pe.wait_ge(ctx_done, at(n, QC, c + 1))
                for t in range(TC):
                    last = nc.tensor.transpose(turn_ps[:, t * P:(t + 1) * P], ctx_sb[c % 2][:, t * P:(t + 1) * P],
                                               ident[:, :])
                last.then_inc(turned, 1)

            def slot(n, key):
                for e in att[key]:
                    if e[0] == "max":
                        max_scores(nxt(n), *e[1:])
                    elif e[0] == "turn_max":
                        turns = [x[1] for x in att[key][:att[key].index(e)] if x[0] == "turn"]
                        pe.wait_ge(ctx_done, at(n, QC, turns[-1] + 2))
                        turn_max(nxt(n))
                    elif e[0] == "turn":
                        before = e[1] < 0
                        if e[1] == -1 or (e[1] == 0 and not key[1]):
                            pe.wait_ge(mt_copied, at(n, 1, 1))
                        turn_context(nxt(n, -1) if before else n, QC - 1 if before else e[1])
                    elif e[0] == "scores":
                        scores(n, *e[1:])
                    elif e[0] == "context":
                        if e[1] < 0:
                            context(nxt(n, -1), NS - 1, *e[2:])
                        else:
                            context(n, *e[1:])

            for m in range(NM):
                max_scores(0, m, *maxes[m])
            turn_max(0)
            slot(0, (True, False))
            with pe.Fori(0, NG // 2 - 1) as i:
                slot((i, 1), (True, True))
                slot((i, 2), (True, True))
            slot(NG - 1, (False, True))
            context(NG - 1, NS - 1, *steps[-1])
            turn_context(NG - 1, QC - 1)
            pe.drain().then_inc(phase_b, 1)
            pe.wait_ge(phase_b, 4)

            def turn_rows(n, half, src):
                pe.wait_ge(tp_copied, at(n, 4, 2 * half + 4))
                for k in range(KC):
                    for t in range(TC):
                        last = nc.tensor.transpose(xt_ps[:, k, t * P:(t + 1) * P], src[:, t, k * P:(k + 1) * P],
                                                   ident[:, :])
                    last.then_inc(tp_ready, 1)

            def attention_out(n):
                pe.wait_ge(cb_ready, at(n, 1, 1))
                turn_rows(n, 0, cb_sb)
                pe.wait_ge(tp_copied, at(n, 4, 6))
                for v in range(2):
                    pe.wait_ge(y_taken, at(n, 2, v + 1))
                    for t in (2 * v, 2 * v + 1):
                        for k in range(KC):
                            last = nc.tensor.matmul(y_ps[v][:, (t % 2) * C:(t % 2 + 1) * C],
                                                    ct_sb[:, k, t * P:(t + 1) * P], wo_sb[:, k, :],
                                                    start=(k == 0), stop=(k == KC - 1))
                    last.then_inc(y_ready, 1)

            def turn_x1(n):
                pe.wait_ge(x1n_ready, at(n, 1, 1))
                turn_rows(n, 1, x1n_sb)

            def mlp_hidden(n):
                pe.wait_ge(tp_copied, at(n, 4, 8))
                for m in range(SM):
                    pe.wait_ge(gelu_done, at(n, SM, m + 1))
                    for k in range(KC):
                        last = nc.tensor.matmul(h_ps[m % 2][:, :], w1_sb[:, k, m * P:(m + 1) * P], x1t_sb[:, k, :],
                                                start=(k == 0), stop=(k == KC - 1))
                    last.then_inc(h_ready, 1)

            def mlp_output(n):
                pe.wait_ge(gelu_done, at(n, SM, SM + 2))
                for v in range(2):
                    pe.wait_ge(f_taken, at(n, 2, v + 1))
                    for t in (2 * v, 2 * v + 1):
                        for m in range(SM):
                            last = nc.tensor.matmul(f_ps[v][:, (t % 2) * C:(t % 2 + 1) * C],
                                                    ht_sb[:, m, t * P:(t + 1) * P], w2_sb[:, m, :],
                                                    start=(m == 0), stop=(m == SM - 1))
                    last.then_inc(f_ready, 1)

            attention_out(0)
            turn_x1(0)

            def chunk(n):
                attention_out(nxt(n))
                mlp_hidden(n)
                turn_x1(nxt(n))
                mlp_output(n)

            with pe.Fori(0, NCH // 2 - 1) as i:
                chunk((i, 0))
                chunk((i, 1))
            chunk(NCH - 2)
            mlp_hidden(NCH - 1)
            mlp_output(NCH - 1)


_INS = ['L0_attn_x', 'L0_attn_W_q', 'L0_attn_W_k', 'L0_attn_W_v', 'L0_attn_W_o', 'L0_attn_b_o',
        'L0_ffn_w1', 'L0_ffn_b1', 'L0_ffn_w2', 'L0_ffn_b2']
_OUTS = [((2, 2048, 256), 'float32')]


def kernel(**inputs):
    import numpy as _np
    import concourse.bacc as _bacc
    from concourse import mybir as _mybir
    from concourse.bass_utils import run_bass_kernel_spmd as _run

    nc = _bacc.Bacc("TRN2", target_bir_lowering=False, num_devices=1)
    arrays, args = {}, []
    for name in _INS:
        a = _np.ascontiguousarray(inputs[name])
        arrays[f"in_{name}_dram"] = a
        args.append(nc.dram_tensor(f"in_{name}_dram", a.shape, _mybir.dt.from_np(a.dtype), kind="ExternalInput").ap())
    for i, (shape, dtype) in enumerate(_OUTS):
        dt = _mybir.dt.from_np(_np.dtype(dtype))
        args.append(nc.dram_tensor(f"out_{i}_dram", shape, dt, kind="ExternalOutput").ap())
    sandwich_kernel(nc, *args)
    r = _run(nc, [arrays], core_ids=[0])
    return r.results[0]["out_0_dram"]
```

```python
from contextlib import ExitStack

import concourse.bass as bass
from concourse import mybir

F32 = mybir.dt.float32
BF16 = mybir.dt.bfloat16
ALU = mybir.AluOpType
ACT = mybir.ActivationFunctionType
AX_X = mybir.AxisListType.X

P = 128
EPS = 1e-5
MASKED = -3.0e38


def at(n, per, plus=0):
    if isinstance(n, tuple):
        i, k = n
        return i * (2 * per) + (k * per + plus)
    return n * per + plus


def parity(n):
    return (n[1] if isinstance(n, tuple) else n) % 2


def nxt(n, k=1):
    return (n[0], n[1] + k) if isinstance(n, tuple) else n + k


def one(n):
    return bass.ds(at(n, 1), 1)


STEP_PATTERN = "SMCSMSMSM"
LAG = 2


def attention_order(tiles_per_chunk, chunks, heads, max_tiles, with_max, pv_before):
    steps = [(c, j) for c in range(chunks) for j in range(tiles_per_chunk * (c + 1))]
    maxes = [(h, t, p) for h in range(heads) for t in range(tiles_per_chunk * chunks)
             for p in range(t // max_tiles + 1)]
    last = len(steps) - 1

    def cols(c, j):
        return tiles_per_chunk - max(0, j - tiles_per_chunk * c)

    def mcols(m):
        _, t, p = m
        return min(max_tiles, t + 1 - max_tiles * p)

    att_total = sum(cols(c, j) for c, j in steps[:last - 2])
    max_total = sum(mcols(m) for m in maxes)
    order, att, mx, m, ended = [], 0, 0, 0, None

    def maxes_up_to(share, at_most):
        nonlocal mx, m
        while with_max and at_most > 0 and m < len(maxes) and mx < share * max_total:
            order.append(("max", m, *maxes[m]))
            mx += mcols(maxes[m])
            m += 1
            at_most -= 1

    for s, (c, j) in enumerate(steps):
        share = (att + cols(c, j)) / att_total
        g = 0
        for what in STEP_PATTERN:
            if what == "S":
                order.append(("scores", s, c, j, g))
                g += 1
            elif what == "M":
                maxes_up_to(share, 1)
            elif s >= LAG or pv_before:
                order.append(("context", s - LAG, *steps[s - LAG]))
        maxes_up_to(share, 9)
        att += cols(c, j)
        done = steps[s - LAG - 1][0]
        if s == LAG and pv_before:
            order.append(("turn", -1))
        elif s > LAG and done != steps[s - LAG][0]:
            order.append(("turn", done))
        if with_max and m == len(maxes):
            ended = s if ended is None else ended
            if s == min(ended + 1, len(steps) - 1):
                order.append(("turn_max",))
                m += 1
    return order, steps, maxes


def sandwich_kernel(nc, x, w_q, w_k, w_v, w_o, b_o, w1, b1, w2, b2, out):
    B, T, C = x.shape
    HEADS, D = 16, C // 16
    S = w1.shape[1]
    CHUNK = 512
    TC = CHUNK // P
    NCH = B * T // CHUNK
    QC = T // CHUNK
    KT = T // P
    KC = C // P
    SM = S // P
    G = 4
    NG = B * HEADS // G
    GC = G * D
    PARTS = 3
    ROWS = 6 * D
    VW = 32
    PB = 4
    assert B == 2 and KC == 2 and QC == 4 and TC == 4

    x_v = x.rearrange("b (q t p) c -> p (b q) t c", t=TC, p=P)
    out_v = out.rearrange("b (q t p) c -> p (b q) t c", t=TC, p=P)
    parts_d = nc.dram_tensor("qk_parts", (2, PARTS, B, C, T), BF16, kind="Internal").ap()

    MT = TC
    RING = 4
    SB = 3
    att, steps, maxes = {}, None, None
    for key in ((True, False), (True, True), (False, True)):
        att[key], steps, maxes = attention_order(TC, QC, G, MT, *key)
    NS = len(steps)
    NM = len(maxes)
    ND = sum(j >= TC * c for c, j in steps)
    NR = NM + QC + 1

    FIRST_USES = [(0, k, k % RING, k + 1) for k in range(NM + 1)]

    def ring_uses(n, key):
        local = int(key == (True, False))
        for e in att[key]:
            if e[0] not in ("max", "turn", "turn_max"):
                yield e, None
                continue
            free = NM + local + 1
            if local < RING:
                uses, base = (NM + 1, 0) if key == (True, False) else (NR, NM - NR)
                free = base + uses - (uses - 1 - local) % RING + RING
            yield e, (n, NM + local, local % RING, free)
            local += 1

    LAST_USE = (NG - 1, NM + QC, QC % RING, NM + QC + 1)
    assert QC >= RING

    ctx = ExitStack()
    with ctx:
        def sb(name, shape, dt):
            return ctx.enter_context(nc.sbuf_tensor(name, shape, dt))

        def psum(name, shape, dt):
            return ctx.enter_context(nc.psum_tensor(name, shape, dt))

        def sem(name):
            return ctx.enter_context(nc.semaphore(name))

        score_ps = [psum(f"score_ps{h}", [P, CHUNK], F32) for h in range(SB)]
        ctx_ps = psum("ctx_ps", [P, CHUNK], F32)
        ring_ps = [psum(f"ring_ps{m}", [P, MT * P], F32) for m in range(RING)]
        xt_ps = ring_ps[0:KC]
        qk_ps = [score_ps[0][:, :], score_ps[1][:, :], score_ps[2][:, :], ctx_ps[:, :]]
        v_ps = [ring_ps[2][:, :], ring_ps[3][:, :]]
        y_ps = v_ps
        h_ps = qk_ps[0:2]
        f_ps = qk_ps[2:4]

        wq_sb = sb("wq_sb", [P, KC, C], F32)
        wk_sb = sb("wk_sb", [P, KC, C], F32)
        wv_sb = sb("wv_sb", [P, KC, C], F32)
        wo_sb = sb("wo_sb", [P, KC, C], F32)
        w1_sb = sb("w1_sb", [P, KC, S], F32)
        w2_sb = sb("w2_sb", [P, SM, C], F32)
        bo_sb = sb("bo_sb", [P, 2, C], F32)
        b2_sb = sb("b2_sb", [P, 2, C], F32)
        b1_sb = sb("b1_sb", [P, SM], F32)
        ident = sb("ident", [P, P], F32)
        ident_bf = sb("ident_bf", [P, P], BF16)
        causal = sb("causal", [P, MT * P], F32)
        stats_sb = sb("stats", [P, 3, TC, 6], F32)
        meanvar_sb = sb("meanvar", [P, 3, TC, 2], F32)
        vareps = sb("vareps", [P, TC], F32)
        rstd = sb("rstd", [P, TC], F32)
        minus_half = sb("minus_half", [P, TC], F32)
        v_all = sb("v_all", [P, NCH, TC, C], F32)
        v_st = [sb(f"v_st{b}", [P, KT, G, VW], F32) for b in range(2)]
        probs = sb("probs", [P, PB, G, CHUNK], F32)
        max_junk = sb("max_junk", [P, RING, MT * P], BF16)
        max_parts = sb("max_parts", [P, G * KT, KT // MT], F32)
        max_q = sb("max_q", [P, G * KT], F32)
        max_rest = sb("max_rest", [P, G * KT], F32)
        max_bf = sb("max_bf", [P, PARTS + 1, G * KT], BF16)
        max_rows = sb("max_rows", [P, 2, P], BF16)
        ctx_sb = [sb(f"ctx_sb{b}", [P, CHUNK], F32) for b in range(2)]
        rden = sb("rden", [P, 2, TC, G], F32)
        arena = sb("arena", [P, 16384], F32)

        stacks = arena[:, :].bitcast(BF16).rearrange("p (b z g t) -> p b z g t", b=2, z=2, g=G)
        q_st = [stacks[:, b, 0] for b in range(2)]
        k_st = [stacks[:, b, 1] for b in range(2)]

        def carve(sizes, dt=F32):
            at_, views = carve.at, []
            for shape in sizes:
                size = 1
                for z in shape:
                    size *= z
                words = size if dt == F32 else size // 2
                v = arena[:, at_:at_ + words]
                if dt != F32:
                    v = v.bitcast(dt)
                if len(shape) == 2:
                    v = v.rearrange("p (a b) -> p a b", a=shape[0])
                views.append(v)
                at_ += words
            carve.at = at_
            assert at_ <= 16384
            return views

        carve.at = 0
        x_sb = carve([(TC, C)] * 2)
        xn_sb = carve([(TC, C)] * 2)
        xt_sb = carve([(KC, CHUNK)] * 2)
        rest_sb = carve([(CHUNK,)] * 4)
        part_sb = carve([(PARTS, CHUNK)] * 4, BF16)
        carve.at = 0
        res_sb = carve([(TC, C)] * 2)
        x1_sb = carve([(TC, C)] * 2)
        o_sb = carve([(TC, C)] * 2)
        cb_sb, = carve([(TC, C)])
        ct_sb, = carve([(KC, CHUNK)])
        yb_sb, = carve([(TC, C)])
        x1n_sb, = carve([(TC, C)])
        x1t_sb, = carve([(KC, CHUNK)])
        fb_sb, = carve([(TC, C)])
        ht_sb, = carve([(SM, CHUNK)])

        w_in = sem("w_in")
        consts = sem("consts")
        x_in = [sem(f"x_in{b}") for b in range(2)]
        ln_a = sem("ln_a")
        xn_ready = sem("xn_ready")
        xt_ready = sem("xt_ready")
        xt_copied = sem("xt_copied")
        qk_ready = sem("qk_ready")
        part1 = sem("part1")
        rest1 = sem("rest1")
        part2 = sem("part2")
        part3 = sem("part3")
        stored = [sem(f"stored{r}") for r in range(4)]
        v_ready = sem("v_ready")
        v_copied = sem("v_copied")
        phase_a = sem("phase_a")
        st_in = [[sem(f"st_in{b}{g}") for g in range(G)] for b in range(2)]
        mrow_in = [sem(f"mrow_in{b}") for b in range(2)]
        ring_ready = sem("ring_ready")
        ring_done = sem("ring_done")
        m_chain = sem("m_chain")
        sc_ready = sem("sc_ready")
        exp_done = sem("exp_done")
        masked = sem("masked")
        pv_done = sem("pv_done")
        vst_ready = sem("vst_ready")
        ctx_copied = sem("ctx_copied")
        rden_done = sem("rden_done")
        phase_b = sem("phase_b")
        res_in = [sem(f"res_in{b}") for b in range(2)]
        res_free = sem("res_free")
        cb_ready = sem("cb_ready")
        tp_ready = sem("tp_ready")
        tp_copied = sem("tp_copied")
        y_ready = sem("y_ready")
        y_taken = sem("y_taken")
        ln_y = sem("ln_y")
        x1_done = sem("x1_done")
        ln_x = sem("ln_x")
        x1n_ready = sem("x1n_ready")
        h_ready = sem("h_ready")
        gelu_done = sem("gelu_done")
        f_ready = sem("f_ready")
        f_taken = sem("f_taken")
        ln_f = sem("ln_f")
        o_ready = sem("o_ready")
        out_done = [sem(f"out_done{b}") for b in range(2)]
        dve_passed = sem("dve_passed")
        pool_passed = sem("pool_passed")
        N_WEIGHTS = 11

        block = ctx.enter_context(nc.Block())

        @block.sync
        def _(sp):
            for b in range(2):
                sp.dma_start(x_sb[b], x_v[:, b]).then_inc(x_in[b], 16)
            for w_sb, w in ((wq_sb, w_q), (wk_sb, w_k), (wv_sb, w_v), (wo_sb, w_o), (w1_sb, w1), (w2_sb, w2)):
                sp.dma_start(w_sb[:, :, :], w.rearrange("(k p) n -> p k n", p=P)).then_inc(w_in, 16)
            for b_sb, b in ((bo_sb, b_o), (b2_sb, b2)):
                for r in range(2):
                    sp.dma_start(b_sb[:, r, :], b.partition_broadcast(P)).then_inc(w_in, 16)
            with nc.allow_non_contiguous_dma(reason="1024 biases, once"):
                sp.dma_start(b1_sb[:, :], b1.rearrange("(m p) -> p m", p=P)).then_inc(w_in, 16)
            for r in range(4):
                sp.sem_inc(stored[r], 16)
            for b in range(2):
                sp.sem_inc(out_done[b], 16)

            def store_parts(n):
                for r in range(4):
                    sp.wait_ge(part3, at(n, 4, r + 1))
                    b, q = n // QC, n % QC
                    dst = parts_d[r // 2, :, b, (r % 2) * P:(r % 2 + 1) * P, q * CHUNK:(q + 1) * CHUNK]
                    sp.dma_start(dst.rearrange("s c t -> c s t"), part_sb[r]).then_inc(stored[r], 16)

            for n in range(NCH):
                store_parts(n)
                if n + 2 < NCH:
                    sp.wait_ge(xn_ready, n + 1)
                    sp.dma_start(x_sb[n % 2], x_v[:, n + 2]).then_inc(x_in[n % 2], 16)
            for r in range(4):
                sp.wait_ge(stored[r], 16 * (NCH + 1))
            sp.wait_ge(phase_a, 4)

            def load_stacks(n, hg, b):
                for g in range(G):
                    q, k = ((parts_d[z, :, b].rearrange("s (h e) t -> s h e t", e=D)[:, bass.ds(hg * G + g, 1)]
                             .rearrange("s h e t -> (s h) e t")) for z in range(2))
                    for r, times in ((0, 3), (1, 2), (2, 1)):
                        at_ = (0, 3, 5)[r]
                        sp.dma_start(q_st[b][at_ * D:(at_ + times) * D, g, :],
                                     q[r:r + 1].to_broadcast([times, D, T])).then_inc(st_in[b][g], 16)
                        sp.dma_start(k_st[b][at_ * D:(at_ + times) * D, g, :], k[0:times]).then_inc(st_in[b][g], 16)

            def load_max_rows(n, use):
                sp.wait_ge(ring_done, at(use[0], NR, use[1] + 1 + RING))
                b = parity(n)
                for s in range(PARTS):
                    dst = q_st[b][ROWS + s:ROWS + s + 1].rearrange("o g (t q) -> o (g t) q", q=P)
                    src = max_rows[(s % 2) * G * KT:(s % 2 + 1) * G * KT, s // 2, :]
                    sp.dma_start(dst, src).then_inc(mrow_in[b], 16)

            load_stacks(0, 0, 0)
            load_stacks(1, 0, 1)
            load_max_rows(0, FIRST_USES[-1])

            def slot(n, key, hg, last=False):
                use, = [u for e, u in ring_uses(n, key) if e[0] == "turn_max"]
                load_max_rows(nxt(n), use)
                if not last:
                    sp.wait_ge(sc_ready, at(n, G * NS, G * NS))
                    load_stacks(nxt(n, 2), hg, parity(n))

            slot(0, (True, False), 1)
            with sp.Fori(0, NG // 2 - 2) as i:
                slot((i, 1), (True, True), i + 1)
                slot((i, 2), (True, True), i + 2)
            slot(NG - 3, (True, True), NG // 2 - 1)
            slot(NG - 2, (True, True), 0, last=True)

            sp.wait_ge(phase_b, 4)
            for b in range(2):
                sp.dma_start(res_sb[b], x_v[:, b]).then_inc(res_in[b], 16)

            def store_out(n):
                sp.wait_ge(o_ready, at(n, 1, 1))
                b = parity(n)
                sp.dma_start(out_v[:, one(n)].rearrange("p o t c -> p (o t) c"), o_sb[b]).then_inc(out_done[b], 16)

            def load_res(n):
                sp.wait_ge(res_free, at(n, 1, -1))
                b = parity(n)
                sp.dma_start(res_sb[b], x_v[:, one(n)].rearrange("p o t c -> p (o t) c")).then_inc(res_in[b], 16)

            with sp.Fori(0, NCH // 2 - 1) as i:
                for k in range(2):
                    load_res((i, k + 2))
                    store_out((i, k))
            for n in (NCH - 2, NCH - 1):
                store_out(n)
            for b in range(2):
                sp.wait_ge(out_done[b], 16 * (NCH // 2 + 1))

        @block.gpsimd
        def _(pool):
            pool.memset(ident[:, :], 0.0)
            pool.memset(ident_bf[:, :], 0.0)
            pool.memset(minus_half[:, :], -0.5)
            pool.memset(causal[:, :], 0.0).then_inc(consts, 1)
            pool.wait_ge(consts, 1)
            pool.affine_select(ident[:, :], ident[:, :], [[-1, P]], ALU.not_equal, 1.0, 0, 1)
            pool.affine_select(ident_bf[:, :], ident_bf[:, :], [[-1, P]], ALU.not_equal, 1.0, 0, 1)
            pool.affine_select(causal[:, (MT - 1) * P:], causal[:, (MT - 1) * P:], [[-1, P]], ALU.is_ge,
                               MASKED, 0, 1).then_inc(consts, 1)
            for b in range(2):
                pool.memset(v_st[b][:, :, :, D:], 0.0)
            pool.memset(max_bf[:, PARTS, :], 0.0)
            pool.memset(max_parts[:, :, :], MASKED).then_inc(consts, 1)
            pool.wait_ge(consts, 3)
            pool.memset(v_st[0][:, :, :, D:D + 1], 1.0)
            pool.memset(v_st[1][:, :, :, D:D + 1], 1.0).then_inc(consts, 1)

            def inverse_root(chain, n, per):
                pool.wait_ge(chain, at(n, per, 3))
                pool.tensor_tensor(rstd[:, :], vareps[:, :], minus_half[:, :], ALU.pow).then_inc(chain, 1)

            with pool.Fori(0, NCH) as n:
                inverse_root(ln_a, n, 4)
            pool.drain().then_inc(phase_a, 1)

            pool.wait_ge(phase_a, 4)
            for b in range(2):
                pool.memset(k_st[b][ROWS:ROWS + PARTS, :, :], 1.0).then_inc(consts, 1)
                pool.wait_ge(consts, 5 + b)

            def stage_values(n, hg, b):
                v = v_all[:, b * QC:(b + 1) * QC, :, :].rearrange("p q t c -> p (q t) c")
                v = v[:, :, bass.ds(hg * GC, GC)].rearrange("p k (g e) -> p k g e", g=G)
                pool.tensor_copy(v_st[b][:, :, :, 0:D], v).then_inc(vst_ready, 1)

            def slot(n, key, hg):
                staged = not key[0]
                for e in att[key]:
                    if e[0] != "scores":
                        continue
                    _, s, c, j, g = e
                    if j < TC * c or g % 2 == 0:
                        continue
                    off = (j - TC * c) * P
                    pool.wait_ge(exp_done, at(n, G * NS, G * s + g + 1 + SB))
                    pool.sem_inc(pool_passed, 1)
                    pr = probs[:, s % PB, g - 1:g + 1, off:off + P]
                    pool.affine_select(pr, pr, [[0, 2], [1, P]], ALU.is_ge, 0.0, 0, -1).then_inc(masked, 1)
                    if s == TC - 1 and g == G - 1 and not staged:
                        if n != 0:
                            pool.wait_ge(pv_done, at(n, NS, PB))
                        stage_values(nxt(n), hg, parity(nxt(n)))

            stage_values(0, 0, 0)
            slot(0, (True, False), 0)
            with pool.Fori(0, NG // 2 - 1) as i:
                slot((i, 1), (True, True), i + 1)
                slot((i, 2), (True, True), i + 1)
            slot(NG - 1, (False, True), 0)
            pool.drain().then_inc(phase_b, 1)
            pool.wait_ge(phase_b, 4)

            def fix_context(n):
                pool.wait_ge(tp_ready, at(n, 4, 2))
                pool.tensor_copy(cb_sb, v_all[:, one(n)].rearrange("p o t c -> p (o t) c")).then_inc(cb_ready, 1)

            def roots_before_mlp(n):
                inverse_root(ln_y, n, 5)
                inverse_root(ln_x, n, 4)

            fix_context(0)
            roots_before_mlp(0)
            fix_context(1)
            with pool.Fori(0, NCH // 2 - 1) as i:
                for k in range(2):
                    roots_before_mlp((i, k + 1))
                    fix_context((i, k + 2))
                    inverse_root(ln_f, (i, k), 5)
            roots_before_mlp(NCH - 1)
            inverse_root(ln_f, NCH - 2, 5)
            inverse_root(ln_f, NCH - 1, 5)

        @block.scalar
        def _(act):
            act.sem_inc(xt_copied, 2)
            act.sem_inc(v_copied, 2)
            act.sem_inc(exp_done, SB)
            act.sem_inc(ctx_copied, 1)
            act.sem_inc(tp_copied, 4)
            act.sem_inc(gelu_done, 2)

            def copy_xt(n):
                for k in range(KC):
                    act.wait_ge(xt_ready, at(n, 2, k + 5))
                    nc.scalar.copy(xt_sb[parity(n)][:, k, :], xt_ps[k][:, :]).then_inc(xt_copied, 1)

            def copy_v(n):
                for v in range(2):
                    act.wait_ge(v_ready, at(n, 2, v + 1))
                    dst = v_all[:, one(n), 2 * v:2 * v + 2, :].rearrange("p o t c -> p (o t c)")
                    nc.scalar.copy(dst, v_ps[v]).then_inc(v_copied, 1)

            def parts_12(n):
                def first(r):
                    act.wait_ge(qk_ready, at(n, 4, r + 1))
                    act.wait_ge(stored[r], at(n, 16, 16))
                    nc.scalar.copy(part_sb[r][:, 0, :], qk_ps[r]).then_inc(part1, 1)

                def second(r):
                    act.wait_ge(rest1, at(n, 4, r + 5))
                    nc.scalar.copy(part_sb[r][:, 1, :], rest_sb[r]).then_inc(part2, 1)

                first(0)
                for r in range(1, 4):
                    first(r)
                    second(r - 1)
                second(3)

            copy_xt(0)
            parts_12(0)
            with act.Fori(0, NCH // 2 - 1) as i:
                for k in (1, 2):
                    copy_xt((i, k))
                    copy_v((i, k - 1))
                    parts_12((i, k))
            copy_xt(NCH - 1)
            copy_v(NCH - 2)
            parts_12(NCH - 1)
            copy_v(NCH - 1)
            act.drain().then_inc(phase_a, 1)
            act.wait_ge(phase_a, 4)

            def copy_context(c):
                nc.scalar.copy(ctx_sb[c % 2][:, :], ctx_ps[:, :]).then_inc(ctx_copied, 1)

            def slot(n, key):
                for e in att[key]:
                    if e[0] == "scores":
                        _, s, c, j, g = e
                        off = max(0, j - TC * c) * P
                        act.wait_ge(sc_ready, at(n, G * NS, G * s + g + 1))
                        if g == 0:
                            act.wait_ge(pv_done, at(n, NS, s + 1))
                        nc.scalar.activation(probs[:, s % PB, g, off:], score_ps[(G * s + g) % SB][:, off:], ACT.Exp,
                                             scale=1.0 / float(D) ** 0.5).then_inc(exp_done, 1)
                    elif e[0] == "context":
                        _, s, c, j = e
                        if j == TC * (c + 1) - 1:
                            act.wait_ge(pv_done, at(n, NS, s + 1 + PB))
                            copy_context(c)

            slot(0, (True, False))
            with act.Fori(0, NG // 2 - 1) as i:
                slot((i, 1), (True, True))
                slot((i, 2), (True, True))
            slot(NG - 1, (False, True))
            act.wait_ge(pv_done, NS * NG + PB)
            copy_context(QC - 1)
            act.drain().then_inc(phase_b, 1)
            act.wait_ge(phase_b, 4)
            act.wait_ge(w_in, 16 * N_WEIGHTS)

            def copy_turned(n, half, dst):
                for k in range(KC):
                    act.wait_ge(tp_ready, at(n, 4, 2 * half + k + 5))
                    if not half:
                        act.wait_ge(y_ready, at(n, 2, 2))
                    nc.scalar.copy(dst[:, k, :], xt_ps[k][:, :]).then_inc(tp_copied, 1)

            def gelu(n):
                act.wait_ge(f_ready, at(n, 2, 2))
                for m in range(SM):
                    act.wait_ge(h_ready, at(n, SM, m + 1))
                    nc.scalar.activation(ht_sb[:, m, :], h_ps[m % 2], ACT.Gelu,
                                         bias=b1_sb[:, m:m + 1]).then_inc(gelu_done, 1)

            copy_turned(0, 0, ct_sb)
            copy_turned(0, 1, x1t_sb)

            def chunk(n):
                copy_turned(nxt(n), 0, ct_sb)
                gelu(n)
                copy_turned(nxt(n), 1, x1t_sb)

            with act.Fori(0, NCH // 2 - 1) as i:
                chunk((i, 0))
                chunk((i, 1))
            chunk(NCH - 2)
            gelu(NCH - 1)

        @block.vector
        def _(dve):
            dve.sem_inc(rest1, 4)
            dve.sem_inc(ring_done, RING)
            dve.sem_inc(y_taken, 2)
            dve.sem_inc(f_taken, 2)

            def layer_norm(src, dst, chain, n, per, kind):
                stats, meanvar = stats_sb[:, kind], meanvar_sb[:, kind]
                for t in range(TC):
                    last = nc.vector.bn_stats(stats[:, t, :], src[:, t, :])
                last.then_inc(chain, 1)
                dve.wait_ge(chain, at(n, per, 1))
                dve.sem_inc(dve_passed, 1)
                for t in range(TC):
                    last = nc.vector.bn_aggr(meanvar[:, t, :], stats[:, t, :])
                last.then_inc(chain, 1)
                dve.wait_ge(chain, at(n, per, 2))
                nc.vector.tensor_scalar(vareps[:, :], meanvar[:, :, 1], EPS, None, ALU.add).then_inc(chain, 1)
                dve.wait_ge(chain, at(n, per, 4))
                for t in range(TC):
                    last = nc.vector.tensor_scalar(dst[:, t, :], src[:, t, :], meanvar[:, t, 0:1], rstd[:, t:t + 1],
                                                   ALU.subtract, ALU.mult)
                return last

            def norm_x(n):
                b = parity(n)
                dve.wait_ge(x_in[b], at(n, 8, 16 - 8 * b))
                dve.wait_ge(xt_ready, at(n, 2, 2))
                layer_norm(x_sb[b], xn_sb[b], ln_a, n, 4, b).then_inc(xn_ready, 1)

            def parts_3(n):
                def rest(r):
                    dve.wait_ge(part1, at(n, 4, r + 1))
                    nc.vector.tensor_tensor(rest_sb[r], qk_ps[r], part_sb[r][:, 0, :],
                                            ALU.subtract).then_inc(rest1, 1)

                def third(r):
                    dve.wait_ge(part2, at(n, 4, r + 1))
                    nc.vector.tensor_tensor(part_sb[r][:, 2, :], rest_sb[r], part_sb[r][:, 1, :],
                                            ALU.subtract).then_inc(part3, 1)

                rest(0)
                for r in range(1, 4):
                    rest(r)
                    third(r - 1)
                third(3)

            norm_x(0)
            norm_x(1)
            parts_3(0)
            with dve.Fori(0, NCH // 2 - 1) as i:
                for k in (1, 2):
                    norm_x((i, k + 1))
                    parts_3((i, k))
            parts_3(NCH - 1)
            dve.drain().then_inc(phase_a, 1)
            dve.wait_ge(phase_a, 4)

            def take_max(use, head, t, p):
                dve.wait_ge(ring_ready, at(use[0], NR, use[1] + 1))
                w = min(MT, t + 1 - MT * p) * P
                dst = max_parts[:, head * KT + t, p:p + 1]
                src = ring_ps[use[2]][:, 0:w]
                if p == t // MT:
                    dve.sem_inc(dve_passed, 1)
                    nc.vector.tensor_tensor_reduce(max_junk[:, use[2], 0:w], src, causal[:, MT * P - w:], 1.0, MASKED,
                                                   ALU.add, ALU.max, dst).then_inc(ring_done, 1)
                else:
                    nc.vector.reduce_max(dst, src, AX_X).then_inc(ring_done, 1)

            def split_max(n, use):
                dve.wait_ge(ring_done, at(use[0], NR, use[1] + RING))
                nc.vector.reduce_max(max_q[:, :], max_parts[:, :, :], AX_X).then_inc(m_chain, 1)
                dve.wait_ge(m_chain, at(n, 5, 1))
                nc.vector.tensor_scalar(max_bf[:, 0, :], max_q[:, :], -1.0, None, ALU.mult).then_inc(m_chain, 1)
                dve.wait_ge(m_chain, at(n, 5, 2))
                nc.vector.scalar_tensor_tensor(max_rest[:, :], max_q[:, :], -1.0, max_bf[:, 0, :],
                                               ALU.mult, ALU.subtract).then_inc(m_chain, 1)
                dve.wait_ge(m_chain, at(n, 5, 3))
                nc.vector.tensor_copy(max_bf[:, 1, :], max_rest[:, :]).then_inc(m_chain, 1)
                dve.wait_ge(m_chain, at(n, 5, 4))
                nc.vector.tensor_tensor(max_bf[:, 2, :], max_rest[:, :], max_bf[:, 1, :],
                                        ALU.subtract).then_inc(m_chain, 1)
                dve.wait_ge(ring_ready, at(use[0], NR, use[1] + 1))
                src = ring_ps[use[2]][:, 0:P].bitcast(BF16).rearrange("p (s q) -> p s q", s=2)
                nc.vector.tensor_copy(max_rows[:, :, :], src).then_inc(ring_done, 1)

            def normalise_context(n, use, c, hg, b):
                turn = ring_ps[use[2]][:, 0:CHUNK].rearrange("p (t g e) -> p t g e", t=TC, g=G)
                dve.wait_ge(ring_ready, at(use[0], NR, use[1] + 1))
                nc.vector.reciprocal(rden[:, c % 2], turn[:, :, :, D]).then_inc(rden_done, 1)
                dve.wait_ge(rden_done, at(n, QC, c + 1))
                dst = v_all[:, b * QC + c, :, bass.ds(hg * GC, GC)].rearrange("p t (g e) -> p t g e", g=G)
                scale = rden[:, c % 2].unsqueeze(3).to_broadcast([P, TC, G, D])
                nc.vector.tensor_tensor(dst, turn[:, :, :, 0:D], scale, ALU.mult).then_inc(ring_done, 1)

            dve.wait_ge(consts, 3)
            for m in range(NM):
                take_max(FIRST_USES[m], *maxes[m])
            split_max(0, FIRST_USES[-1])

            def slot(n, key, hg, hg_before):
                for e, use in ring_uses(n, key):
                    if e[0] == "max":
                        take_max(use, *e[2:])
                    elif e[0] == "turn_max":
                        split_max(nxt(n), use)
                    elif e[0] == "turn":
                        if e[1] < 0:
                            normalise_context(nxt(n, -1), use, QC - 1, hg_before, parity(nxt(n, -1)))
                        else:
                            normalise_context(n, use, e[1], hg, parity(n))

            slot(0, (True, False), 0, 0)
            with dve.Fori(0, NG // 2 - 1) as i:
                slot((i, 1), (True, True), i, i)
                slot((i, 2), (True, True), i + 1, i)
            slot(NG - 1, (False, True), NG // 2 - 1, NG // 2 - 1)
            normalise_context(NG - 1, LAST_USE, QC - 1, NG // 2 - 1, 1)
            dve.drain().then_inc(phase_b, 1)
            dve.wait_ge(phase_b, 4)
            dve.wait_ge(w_in, 16 * N_WEIGHTS)

            def attention_out(n):
                b = parity(n)
                for v in range(2):
                    dve.wait_ge(y_ready, at(n, 2, v + 3))
                    nc.vector.tensor_tensor(yb_sb[:, 2 * v:2 * v + 2, :],
                                            y_ps[v].rearrange("p (t c) -> p t c", t=2), bo_sb[:, :, :],
                                            ALU.add).then_inc(y_taken, 1)
                dve.wait_ge(y_taken, at(n, 2, 4))
                layer_norm(yb_sb, yb_sb, ln_y, n, 5, 0).then_inc(ln_y, 1)
                dve.wait_ge(ln_y, at(n, 5, 5))
                dve.wait_ge(res_in[b], at(n, 8, 16 - 8 * b))
                nc.vector.tensor_tensor(x1_sb[b], yb_sb, res_sb[b], ALU.add).then_inc(res_free, 1)
                dve.wait_ge(res_free, at(n, 1, 1))
                dve.wait_ge(tp_ready, at(n, 4, 4))
                layer_norm(x1_sb[b], x1n_sb, ln_x, n, 4, 1).then_inc(x1n_ready, 1)

            def mlp_out(n):
                b = parity(n)
                for v in range(2):
                    dve.wait_ge(f_ready, at(n, 2, v + 3))
                    nc.vector.tensor_tensor(fb_sb[:, 2 * v:2 * v + 2, :],
                                            f_ps[v].rearrange("p (t c) -> p t c", t=2), b2_sb[:, :, :],
                                            ALU.add).then_inc(f_taken, 1)
                dve.wait_ge(f_taken, at(n, 2, 4))
                layer_norm(fb_sb, fb_sb, ln_f, n, 5, 2).then_inc(ln_f, 1)
                dve.wait_ge(ln_f, at(n, 5, 5))
                dve.wait_ge(out_done[b], at(n, 8, 16 - 8 * b))
                nc.vector.tensor_tensor(o_sb[b], fb_sb, x1_sb[b], ALU.add).then_inc(o_ready, 1)

            attention_out(0)

            def chunk(n):
                attention_out(nxt(n))
                mlp_out(n)

            with dve.Fori(0, NCH // 2 - 1) as i:
                chunk((i, 0))
                chunk((i, 1))
            chunk(NCH - 2)
            dve.wait_ge(o_ready, NCH - 1)
            mlp_out(NCH - 1)

        @block.tensor
        def _(pe):
            pe.sem_inc(xt_ready, 4)
            pe.sem_inc(pv_done, PB)
            pe.sem_inc(tp_ready, 4)
            pe.sem_inc(y_ready, 2)
            pe.sem_inc(f_ready, 2)
            pe.wait_ge(consts, 2)
            pe.wait_ge(w_in, 16 * N_WEIGHTS)

            def turn_x(n):
                pe.wait_ge(xn_ready, at(n, 1, 1))
                pe.wait_ge(xt_copied, at(n, 2, 2))
                for k in range(KC):
                    for t in range(TC):
                        last = nc.tensor.transpose(xt_ps[k][:, t * P:(t + 1) * P],
                                                   xn_sb[parity(n)][:, t, k * P:(k + 1) * P], ident[:, :])
                    last.then_inc(xt_ready, 1)

            def project_v(n):
                for v in range(2):
                    pe.wait_ge(v_copied, at(n, 2, v + 1))
                    for t in (2 * v, 2 * v + 1):
                        for k in range(KC):
                            last = nc.tensor.matmul(v_ps[v][:, (t % 2) * C:(t % 2 + 1) * C],
                                                    xt_sb[parity(n)][:, k, t * P:(t + 1) * P], wv_sb[:, k, :],
                                                    start=(k == 0), stop=(k == KC - 1))
                    last.then_inc(v_ready, 1)

            def project_qk(n):
                pe.wait_ge(xt_copied, at(n, 2, 4))
                for r in range(4):
                    w = (wq_sb, wk_sb)[r // 2]
                    pe.wait_ge(rest1, at(n, 4, r + 1))
                    for k in range(KC):
                        last = nc.tensor.matmul(qk_ps[r], w[:, k, (r % 2) * P:(r % 2 + 1) * P],
                                                xt_sb[parity(n)][:, k, :], start=(k == 0), stop=(k == KC - 1))
                    last.then_inc(qk_ready, 1)

            turn_x(0)
            project_qk(0)
            with pe.Fori(0, NCH // 2 - 1) as i:
                for k in (1, 2):
                    turn_x((i, k))
                    project_v((i, k - 1))
                    project_qk((i, k))
            turn_x(NCH - 1)
            project_v(NCH - 2)
            project_qk(NCH - 1)
            project_v(NCH - 1)
            pe.drain().then_inc(phase_a, 1)
            pe.wait_ge(phase_a, 4)
            pe.wait_ge(consts, 6)

            def max_scores(n, use, head, t, p):
                b = parity(n)
                if t == 0:
                    pe.wait_ge(st_in[b][head], at(n, 48, 96 - 48 * b))
                pe.wait_ge(ring_done, at(use[0], NR, use[3]))
                w = min(MT, t + 1 - MT * p) * P
                for a in range(0, w, CHUNK):
                    z = min(w, a + CHUNK)
                    last = nc.tensor.matmul(ring_ps[use[2]][:, a:z], q_st[b][0:ROWS, head, t * P:(t + 1) * P],
                                            k_st[b][0:ROWS, head, p * MT * P + a:p * MT * P + z],
                                            start=True, stop=True)
                last.then_inc(ring_ready, 1)

            def turn_max(n, use):
                pe.wait_ge(ring_done, at(use[0], NR, use[3]))
                pe.wait_ge(m_chain, at(n, 5, 5))
                dst = ring_ps[use[2]][:, 0:P].bitcast(BF16)
                for s in range(2):
                    last = nc.tensor.transpose(dst[:, s * P:(s + 1) * P],
                                               max_bf[:, 2 * s:2 * s + 2, :].rearrange("p s m -> p (s m)"),
                                               ident_bf[:, :])
                last.then_inc(ring_ready, 1)

            def scores(n, s, c, j, g):
                b = parity(n)
                off = max(0, j - TC * c) * P
                if s == 0 and g == 0:
                    pe.wait_ge(mrow_in[b], at(n, 24, 48 - 24 * b))
                u = G * s + g
                if u >= SB:
                    pe.wait_ge(exp_done, at(n, G * NS, u + 1))
                else:
                    pe.wait_ge(exp_done, at(n, G * NS, SB - (G * NS - 1 - u) % SB))
                nc.tensor.matmul(score_ps[u % SB][:, off:],
                                 k_st[b][0:ROWS + PARTS, g, j * P:(j + 1) * P],
                                 q_st[b][0:ROWS + PARTS, g, c * CHUNK + off:(c + 1) * CHUNK],
                                 start=True, stop=True).then_inc(sc_ready, 1)

            def context(n, s, c, j):
                off = max(0, j - TC * c) * P
                if s == 0:
                    pe.wait_ge(vst_ready, at(n, 1, 1))
                if j == 0:
                    pe.wait_ge(ctx_copied, at(n, QC, c + 1))
                pe.wait_ge(exp_done, at(n, G * NS, G * s + G + SB))
                if j >= TC * c:
                    pe.wait_ge(masked, at(n, 2 * ND, 2 * (TC * c + j - TC * c) + 2))
                for g in range(G):
                    last = nc.tensor.matmul(ctx_ps[g * VW:(g + 1) * VW, off:], v_st[parity(n)][:, j, g, :],
                                            probs[:, s % PB, g, off:], start=(j == 0), stop=(j == TC * (c + 1) - 1))
                last.then_inc(pv_done, 1)

            def turn_context(n, use, c):
                pe.wait_ge(ctx_copied, at(n, QC, c + 2))
                pe.wait_ge(ring_done, at(use[0], NR, use[3]))
                for t in range(TC):
                    last = nc.tensor.transpose(ring_ps[use[2]][:, t * P:(t + 1) * P],
                                               ctx_sb[c % 2][:, t * P:(t + 1) * P], ident[:, :])
                last.then_inc(ring_ready, 1)

            def slot(n, key):
                for e, use in ring_uses(n, key):
                    if e[0] == "max":
                        max_scores(nxt(n), use, *e[2:])
                    elif e[0] == "turn_max":
                        turn_max(nxt(n), use)
                    elif e[0] == "turn":
                        if e[1] < 0:
                            turn_context(nxt(n, -1), use, QC - 1)
                        else:
                            turn_context(n, use, e[1])
                    elif e[0] == "scores":
                        scores(n, *e[1:])
                    elif e[0] == "context":
                        if e[1] < 0:
                            context(nxt(n, -1), NS + e[1], *e[2:])
                        else:
                            context(n, *e[1:])

            for m in range(NM):
                max_scores(0, FIRST_USES[m], *maxes[m])
            turn_max(0, FIRST_USES[-1])
            slot(0, (True, False))
            with pe.Fori(0, NG // 2 - 1) as i:
                slot((i, 1), (True, True))
                slot((i, 2), (True, True))
            slot(NG - 1, (False, True))
            for s in range(NS - LAG, NS):
                context(NG - 1, s, *steps[s])
            turn_context(NG - 1, LAST_USE, QC - 1)
            pe.drain().then_inc(phase_b, 1)
            pe.wait_ge(phase_b, 4)

            def turn_rows(n, half, src):
                pe.wait_ge(tp_copied, at(n, 4, 2 * half + 4))
                for k in range(KC):
                    for t in range(TC):
                        last = nc.tensor.transpose(xt_ps[k][:, t * P:(t + 1) * P], src[:, t, k * P:(k + 1) * P],
                                                   ident[:, :])
                    last.then_inc(tp_ready, 1)

            def attention_out(n):
                pe.wait_ge(cb_ready, at(n, 1, 1))
                turn_rows(n, 0, cb_sb)
                pe.wait_ge(tp_copied, at(n, 4, 6))
                for v in range(2):
                    pe.wait_ge(y_taken, at(n, 2, v + 1))
                    for t in (2 * v, 2 * v + 1):
                        for k in range(KC):
                            last = nc.tensor.matmul(y_ps[v][:, (t % 2) * C:(t % 2 + 1) * C],
                                                    ct_sb[:, k, t * P:(t + 1) * P], wo_sb[:, k, :],
                                                    start=(k == 0), stop=(k == KC - 1))
                    last.then_inc(y_ready, 1)

            def turn_x1(n):
                pe.wait_ge(x1n_ready, at(n, 1, 1))
                turn_rows(n, 1, x1n_sb)

            def mlp_hidden(n):
                pe.wait_ge(tp_copied, at(n, 4, 8))
                for m in range(SM):
                    pe.wait_ge(gelu_done, at(n, SM, m + 1))
                    for k in range(KC):
                        last = nc.tensor.matmul(h_ps[m % 2], w1_sb[:, k, m * P:(m + 1) * P], x1t_sb[:, k, :],
                                                start=(k == 0), stop=(k == KC - 1))
                    last.then_inc(h_ready, 1)

            def mlp_output(n):
                pe.wait_ge(gelu_done, at(n, SM, SM + 2))
                for v in range(2):
                    pe.wait_ge(f_taken, at(n, 2, v + 1))
                    for t in (2 * v, 2 * v + 1):
                        for m in range(SM):
                            last = nc.tensor.matmul(f_ps[v][:, (t % 2) * C:(t % 2 + 1) * C],
                                                    ht_sb[:, m, t * P:(t + 1) * P], w2_sb[:, m, :],
                                                    start=(m == 0), stop=(m == SM - 1))
                    last.then_inc(f_ready, 1)

            attention_out(0)
            turn_x1(0)

            def chunk(n):
                attention_out(nxt(n))
                mlp_hidden(n)
                turn_x1(nxt(n))
                mlp_output(n)

            with pe.Fori(0, NCH // 2 - 1) as i:
                chunk((i, 0))
                chunk((i, 1))
            chunk(NCH - 2)
            mlp_hidden(NCH - 1)
            mlp_output(NCH - 1)


_INS = ['L0_attn_x', 'L0_attn_W_q', 'L0_attn_W_k', 'L0_attn_W_v', 'L0_attn_W_o', 'L0_attn_b_o',
        'L0_ffn_w1', 'L0_ffn_b1', 'L0_ffn_w2', 'L0_ffn_b2']
_OUTS = [((2, 2048, 256), 'float32')]


def kernel(**inputs):
    import numpy as _np
    import concourse.bacc as _bacc
    from concourse import mybir as _mybir
    from concourse.bass_utils import run_bass_kernel_spmd as _run

    nc = _bacc.Bacc("TRN2", target_bir_lowering=False, num_devices=1)
    arrays, args = {}, []
    for name in _INS:
        a = _np.ascontiguousarray(inputs[name])
        arrays[f"in_{name}_dram"] = a
        args.append(nc.dram_tensor(f"in_{name}_dram", a.shape, _mybir.dt.from_np(a.dtype), kind="ExternalInput").ap())
    for i, (shape, dtype) in enumerate(_OUTS):
        dt = _mybir.dt.from_np(_np.dtype(dtype))
        args.append(nc.dram_tensor(f"out_{i}_dram", shape, dt, kind="ExternalOutput").ap())
    sandwich_kernel(nc, *args)
    r = _run(nc, [arrays], core_ids=[0])
    return r.results[0]["out_0_dram"]
```

```python
from contextlib import ExitStack

import concourse.bass as bass
from concourse import mybir

F32 = mybir.dt.float32
F32R = mybir.dt.float32r
BF16 = mybir.dt.bfloat16
ALU = mybir.AluOpType
ACT = mybir.ActivationFunctionType
AX_X = mybir.AxisListType.X

P = 128
EPS = 1e-5
MASKED = -3.0e38


def at(n, per, plus=0):
    if isinstance(n, tuple):
        i, k = n
        return i * (2 * per) + (k * per + plus)
    return n * per + plus


def parity(n):
    return (n[1] if isinstance(n, tuple) else n) % 2


def nxt(n, k=1):
    return (n[0], n[1] + k) if isinstance(n, tuple) else n + k


def one(n):
    return bass.ds(at(n, 1), 1)


STEP_PATTERN = "SMCSMSMSM"
LAG = 2
LEAD = 0.51
TURN_AFTER = 8


def attention_order(tiles_per_chunk, chunks, heads, max_tiles, last, pv_before):
    steps = [(c, j) for c in range(chunks) for j in range(tiles_per_chunk * (c + 1))]

    def cols(c, j):
        return tiles_per_chunk - max(0, j - tiles_per_chunk * c)

    def mcols(t, p):
        return min(max_tiles, t + 1 - max_tiles * p)

    stream, done, turns = [], 0, []
    for c in range(chunks):
        for h in range(heads):
            for t in range(tiles_per_chunk * c, tiles_per_chunk * (c + 1)):
                for p in range(t // max_tiles + 1):
                    done += mcols(t, p)
                    stream.append((done, "max", h, t, p))
                    turns = [(left - 1, e) for left, e in turns]
                    while turns and turns[0][0] == 0:
                        stream.append((done, "turn_max", turns.pop(0)[1]))
        stream.append((done, "split", c))
        turns.append((TURN_AFTER, c))
    total = done
    stream = [(d / total, *e) for d, *e in stream]
    late = [(1 + stream[TURN_AFTER - 1][0], "turn_max", turns[0][1])]
    now = [(d - LEAD, e[0], 0, *e[1:]) for d, *e in stream + late if d > LEAD]
    then = [(d + 1 - LEAD, e[0], 1, *e[1:]) for d, *e in stream if d <= LEAD]
    todo = sorted(now + ([] if last else then), key=lambda e: e[0])

    att_total = sum(cols(c, j) for c, j in steps[:-1])
    order, att = [], 0

    def maxes_up_to(share, at_most):
        while at_most > 0 and todo and todo[0][0] <= share:
            at_most -= todo[0][1] == "max"
            order.append(todo.pop(0)[1:])

    for s, (c, j) in enumerate(steps):
        share = (att + cols(c, j)) / att_total
        g = 0
        for what in STEP_PATTERN:
            if what == "S":
                order.append(("scores", s, c, j, g))
                g += 1
            elif what == "M":
                maxes_up_to(share, 1)
            elif s >= LAG or pv_before:
                order.append(("context", s - LAG, *steps[s - LAG]))
        maxes_up_to(share if s < len(steps) - 1 else 2, 99)
        att += cols(c, j)
        done = steps[s - LAG - 1][0]
        if s == LAG and pv_before:
            order.append(("turn", -1))
        elif s > LAG and done != steps[s - LAG][0]:
            order.append(("turn", done))
    return order, steps


def sandwich_kernel(nc, x, w_q, w_k, w_v, w_o, b_o, w1, b1, w2, b2, out):
    B, T, C = x.shape
    HEADS, D = 16, C // 16
    S = w1.shape[1]
    CHUNK = 512
    TC = CHUNK // P
    NCH = B * T // CHUNK
    QC = T // CHUNK
    KT = T // P
    KC = C // P
    SM = S // P
    G = 4
    NG = B * HEADS // G
    GC = G * D
    PARTS = 3
    ROWS = 6 * D
    VW = 32
    PB = 4
    GB = 4
    assert B == 2 and KC == 2 and QC == 4 and TC == 4

    x_v = x.rearrange("b (q t p) c -> p (b q) t c", t=TC, p=P)
    out_v = out.rearrange("b (q t p) c -> p (b q) t c", t=TC, p=P)
    parts_d = nc.dram_tensor("qk_parts", (2, PARTS, B, C, T), BF16, kind="Internal").ap()

    MT = TC
    RING = 4
    SB = 3
    att, steps = {}, None
    for key in ((False, False), (True, False), (True, True)):
        att[key], steps = attention_order(TC, QC, G, MT, key[1], key[0])
    FIRST_ORDER = [(e[0], 0, *e[2:]) for e in att[True, False] if e[0] in ("max", "split", "turn_max") and e[1]]
    NS = len(steps)
    ND = sum(j >= TC * c for c, j in steps)

    def count_uses(order):
        return sum(e[0] in ("max", "turn", "turn_max") for e in order)

    NR = count_uses(att[True, False])
    NF = count_uses(FIRST_ORDER)

    def first_uses():
        uses = 0
        for e in FIRST_ORDER:
            yield e, None if e[0] == "split" else (0, uses, uses % RING, uses + 1)
            uses += e[0] != "split"

    def ring_uses(n, key):
        local = int(not key[0])
        for e in att[key]:
            if e[0] not in ("max", "turn", "turn_max"):
                yield e, None
                continue
            free = NF + local
            if local < RING:
                uses, base = (NR, NF - 1 - NR) if key[0] else (NF, 0)
                free = base + uses - (uses - 1 - local) % RING + RING
            yield e, (n, NF - 1 + local, local % RING, free)
            local += 1

    LAST_USES = count_uses(att[True, True])
    LAST_USE = (NG - 1, NF - 1 + LAST_USES, LAST_USES % RING, NF + LAST_USES)
    assert LAST_USES >= RING

    ctx = ExitStack()
    with ctx:
        def sb(name, shape, dt):
            return ctx.enter_context(nc.sbuf_tensor(name, shape, dt))

        def psum(name, shape, dt):
            return ctx.enter_context(nc.psum_tensor(name, shape, dt))

        def sem(name):
            return ctx.enter_context(nc.semaphore(name))

        score_ps = [psum(f"score_ps{h}", [P, CHUNK], F32) for h in range(SB)]
        ctx_ps = psum("ctx_ps", [P, CHUNK], F32)
        ring_ps = [psum(f"ring_ps{m}", [P, MT * P], F32) for m in range(RING)]
        xt_ps = ring_ps[0:KC]
        qk_ps = [score_ps[0][:, :], score_ps[1][:, :], score_ps[2][:, :], ctx_ps[:, :]]
        v_ps = [ring_ps[2][:, :], ring_ps[3][:, :]]
        y_ps = v_ps
        h_ps = qk_ps[0:2]
        f_ps = qk_ps[2:4]

        wo_sb = sb("wo_sb", [P, KC, C], F32)
        w1_sb = sb("w1_sb", [P, KC, S], F32)
        w2_sb = sb("w2_sb", [P, SM, C], F32)
        bo_sb = sb("bo_sb", [P, 2, C], F32)
        b2_sb = sb("b2_sb", [P, 2, C], F32)
        b1_sb = sb("b1_sb", [P, SM], F32)
        ident = sb("ident", [P, P], F32)
        ident_bf = sb("ident_bf", [P, P], BF16)
        causal = sb("causal", [P, MT * P], F32)
        stats_sb = sb("stats", [P, 3, TC, 6], F32)
        meanvar_sb = sb("meanvar", [P, 3, TC, 2], F32)
        vareps = sb("vareps", [P, TC], F32)
        rstd = sb("rstd", [P, TC], F32)
        minus_half = sb("minus_half", [P, TC], F32)
        v_all = sb("v_all", [P, NCH, TC, C], F32)
        max_parts = sb("max_parts", [P, 2, G * TC, QC], F32)
        max_q = sb("max_q", [P, G * TC], F32)
        max_rest = sb("max_rest", [P, G * TC], F32)
        max_bf = sb("max_bf", [P, P // (G * TC), G * TC], BF16)
        max_rows = sb("max_rows", [P, P], BF16)
        ctx_sb = [sb(f"ctx_sb{b}", [P, CHUNK], F32) for b in range(2)]
        rden = sb("rden", [P, 2, TC, G], F32)

        early, first = ExitStack(), ExitStack()

        def sb_in(scope, name, shape, dt):
            return scope.enter_context(nc.sbuf_tensor(name, shape, dt))

        v_st = [sb_in(early, f"v_st{b}", [P, KT, G, VW], F32) for b in range(2)]
        max_junk = sb_in(early, "max_junk", [P, RING, MT * P], BF16)
        stacks = [sb_in(early, "stack0", [P, 2, G, T], BF16)]

        wqkv_sb = [sb_in(first, f"{w}_sb", [P, KC, C], F32) for w in ("wq", "wk", "wv")]
        wqkv_hi = [sb_in(first, f"{w}_hi", [P, KC, C], F32R) for w in ("wq", "wk", "wv")]
        wqkv_lo = [sb_in(first, f"{w}_lo", [P, KC, C], F32R) for w in ("wq", "wk", "wv")]
        x_sb = [sb_in(first, f"x_sb{b}", [P, TC, C], F32) for b in range(2)]
        xn_sb = [sb_in(first, f"xn_sb{b}", [P, TC, C], F32) for b in range(2)]
        xt_hi = [sb_in(first, f"xt_hi{b}", [P, KC, CHUNK], F32R) for b in range(2)]
        xt_lo = [sb_in(first, f"xt_lo{b}", [P, KC, CHUNK], F32R) for b in range(2)]
        rest_sb = [sb_in(first, f"rest_sb{r}", [P, CHUNK], F32) for r in range(4)]
        part_sb = [sb_in(first, f"part_sb{r}", [P, PARTS, CHUNK], BF16) for r in range(4)]
        first.close()

        probs = sb_in(early, "probs", [P, PB, G, CHUNK], F32)
        stacks.append(sb_in(early, "stack1", [P, 2, G, T], BF16))
        q_st = [stack[:, 0].rearrange("p g t -> p (g t)").rearrange("p (c g t) -> p c g t", c=QC, g=G)
                for stack in stacks]
        k_st = [stack[:, 1] for stack in stacks]
        early.close()

        res_sb = [sb(f"res_sb{b}", [P, TC, C], F32)[:, :, :] for b in range(2)]
        x1_sb = [sb(f"x1_sb{b}", [P, TC, C], F32)[:, :, :] for b in range(2)]
        o_sb = [sb(f"o_sb{b}", [P, TC, C], F32)[:, :, :] for b in range(2)]
        cb_sb, yb_sb, fb_sb, x1n_sb = (sb(name, [P, TC, C], F32)[:, :, :]
                                       for name in ("cb_sb", "yb_sb", "fb_sb", "x1n_sb"))
        ct_sb = sb("ct_sb", [P, KC, CHUNK], F32)
        gelu_sb = [sb(f"gelu_sb{b}", [P, CHUNK], F32)[:, :] for b in range(GB)]
        x1t_hi, x1t_lo = (sb(name, [P, KC, CHUNK], F32R) for name in ("x1t_hi", "x1t_lo"))
        ht_hi, ht_lo = (sb(name, [P, SM, CHUNK], F32R) for name in ("ht_hi", "ht_lo"))
        w1_hi, w1_lo = (sb(name, [P, KC, S], F32R) for name in ("w1_hi", "w1_lo"))
        w2_hi, w2_lo = (sb(name, [P, SM, C], F32R) for name in ("w2_hi", "w2_lo"))

        qkv_in = sem("qkv_in")
        w_in = sem("w_in")
        consts = sem("consts")
        x_in = [sem(f"x_in{b}") for b in range(2)]
        ln_a = sem("ln_a")
        xn_ready = sem("xn_ready")
        xt_ready = sem("xt_ready")
        qkv_hi = sem("qkv_hi")
        qkv_lo = sem("qkv_lo")
        xt_high = sem("xt_high")
        xt_low = sem("xt_low")
        qk_ready = sem("qk_ready")
        part1 = sem("part1")
        rest1 = sem("rest1")
        part2 = sem("part2")
        part3 = sem("part3")
        stored = [sem(f"stored{r}") for r in range(4)]
        v_ready = sem("v_ready")
        v_copied = sem("v_copied")
        phase_a = sem("phase_a")
        st_in = [[sem(f"st_in{b}{g}") for g in range(G)] for b in range(2)]
        mrow_in = sem("mrow_in")
        ring_ready = sem("ring_ready")
        ring_done = sem("ring_done")
        m_chain = sem("m_chain")
        sc_ready = sem("sc_ready")
        exp_done = sem("exp_done")
        masked = sem("masked")
        pv_done = sem("pv_done")
        vst_ready = sem("vst_ready")
        ctx_copied = sem("ctx_copied")
        rden_done = sem("rden_done")
        phase_b = sem("phase_b")
        res_in = [sem(f"res_in{b}") for b in range(2)]
        res_free = sem("res_free")
        w_hi = sem("w_hi")
        w1_low = sem("w1_low")
        w2_low = sem("w2_low")
        cb_ready = sem("cb_ready")
        ct_ready = sem("ct_ready")
        ct_copied = sem("ct_copied")
        y_ready = sem("y_ready")
        y_taken = sem("y_taken")
        ln_y = sem("ln_y")
        ln_x = sem("ln_x")
        x1n_ready = sem("x1n_ready")
        x1t_ready = sem("x1t_ready")
        x1t_high = sem("x1t_high")
        x1t_low = sem("x1t_low")
        h_ready = sem("h_ready")
        gelu_done = sem("gelu_done")
        gelu_low = sem("gelu_low")
        f_ready = sem("f_ready")
        f_taken = sem("f_taken")
        ln_f = sem("ln_f")
        o_ready = sem("o_ready")
        out_done = [sem(f"out_done{b}") for b in range(2)]
        dve_passed = sem("dve_passed")
        pool_passed = sem("pool_passed")
        N_WEIGHTS = 8

        block = ctx.enter_context(nc.Block())

        @block.sync
        def _(sp):
            sp.dma_start(x_sb[0][:, :, :], x_v[:, 0]).then_inc(x_in[0], 16)
            for w_sb, w in zip(wqkv_sb, (w_q, w_k, w_v)):
                sp.dma_start(w_sb[:, :, :], w.rearrange("(k p) n -> p k n", p=P)).then_inc(qkv_in, 16)
            sp.dma_start(x_sb[1][:, :, :], x_v[:, 1]).then_inc(x_in[1], 16)
            for w_sb, w in ((wo_sb, w_o), (w1_sb, w1), (w2_sb, w2)):
                sp.dma_start(w_sb[:, :, :], w.rearrange("(k p) n -> p k n", p=P)).then_inc(w_in, 16)
            for b_sb, b in ((bo_sb, b_o), (b2_sb, b2)):
                for r in range(2):
                    sp.dma_start(b_sb[:, r, :], b.partition_broadcast(P)).then_inc(w_in, 16)
            with nc.allow_non_contiguous_dma(reason="1024 biases, once"):
                sp.dma_start(b1_sb[:, :], b1.rearrange("(m p) -> p m", p=P)).then_inc(w_in, 16)
            for r in range(4):
                sp.sem_inc(stored[r], 16)
            for b in range(2):
                sp.sem_inc(out_done[b], 16)

            def store_parts(n, r):
                sp.wait_ge(part3, at(n, 4, r + 1))
                b, q = n // QC, n % QC
                dst = parts_d[r // 2, :, b, (r % 2) * P:(r % 2 + 1) * P, q * CHUNK:(q + 1) * CHUNK]
                sp.dma_start(dst.rearrange("s c t -> c s t"), part_sb[r][:, :, :]).then_inc(stored[r], 16)

            def load_stack(hg, b, g):
                q, k = ((parts_d[z, :, b].rearrange("s (h e) t -> s h e t", e=D)[:, bass.ds(hg * G + g, 1)]
                         .rearrange("s h e t -> (s h) e t")) for z in range(2))
                q_row = 0
                for r, times in ((0, 3), (1, 2), (2, 1)):
                    at_ = (0, 3, 5)[r]
                    sp.dma_start(k_st[b][at_ * D:(at_ + times) * D, g, :], k[0:times]).then_inc(st_in[b][g], 16)
                    for _ in range(times):
                        sp.dma_start(q_st[b][q_row:q_row + D, :, g, :],
                                     q[r].rearrange("e (c t) -> e c t", c=QC)).then_inc(st_in[b][g], 16)
                        q_row += D

            for n in range(NCH):
                if n + 2 < NCH:
                    sp.wait_ge(xn_ready, n + 1)
                    sp.dma_start(x_sb[n % 2][:, :, :], x_v[:, n + 2]).then_inc(x_in[n % 2], 16)
                for r in range(4):
                    store_parts(n, r)
                    if n == QC:
                        sp.wait_ge(stored[r], 16 * (QC + 1))
                    elif QC < n < QC + 3 and r < 2:
                        load_stack(0, 0, 2 * (n - QC - 1) + r)
            for r in range(4):
                sp.wait_ge(stored[r], 16 * (NCH + 1))
            sp.wait_ge(phase_a, 4)

            def load_stacks(hg, b):
                for g in range(G):
                    load_stack(hg, b, g)

            def load_max_rows(n, use, c):
                sp.wait_ge(ring_done, at(use[0], NR, use[1] + 1 + RING))
                b = parity(n)
                for s in range(PARTS):
                    dst = q_st[b][ROWS + s:ROWS + s + 1, c]
                    src = max_rows[s * G * TC:(s + 1) * G * TC, :]
                    sp.dma_start(dst.rearrange("o g (t q) -> o (g t) q", q=P), src).then_inc(mrow_in, 16)

            load_stacks(0, 1)
            for e, use in first_uses():
                if e[0] == "turn_max":
                    load_max_rows(0, use, e[2])

            def slot(n, key, hg_next=None):
                if hg_next is not None:
                    sp.wait_ge(sc_ready, at(n, G * NS))
                    load_stacks(hg_next, parity(nxt(n)))
                for e, use in ring_uses(n, key):
                    if e[0] == "turn_max":
                        load_max_rows(nxt(n, e[1]), use, e[2])

            slot(0, (False, False))
            with sp.Fori(0, NG // 2 - 1) as i:
                slot((i, 1), (True, False), i + 1)
                slot((i, 2), (True, False), i + 1)
            slot(NG - 1, (True, True))

            sp.wait_ge(phase_b, 4)
            for b in range(2):
                sp.dma_start(res_sb[b], x_v[:, b]).then_inc(res_in[b], 16)

            def store_out(n):
                sp.wait_ge(o_ready, at(n, 1, 1))
                b = parity(n)
                sp.dma_start(out_v[:, one(n)].rearrange("p o t c -> p (o t) c"), o_sb[b]).then_inc(out_done[b], 16)

            def load_res(n):
                sp.wait_ge(res_free, at(n, 1, -1))
                b = parity(n)
                sp.dma_start(res_sb[b], x_v[:, one(n)].rearrange("p o t c -> p (o t) c")).then_inc(res_in[b], 16)

            with sp.Fori(0, NCH // 2 - 1) as i:
                for k in range(2):
                    load_res((i, k + 2))
                    store_out((i, k))
            for n in (NCH - 2, NCH - 1):
                store_out(n)
            for b in range(2):
                sp.wait_ge(out_done[b], 16 * (NCH // 2 + 1))

        @block.gpsimd
        def _(pool):
            pool.memset(ident[:, :], 0.0)
            pool.memset(ident_bf[:, :], 0.0)
            pool.memset(minus_half[:, :], -0.5)
            pool.memset(causal[:, :], 0.0).then_inc(consts, 1)
            pool.wait_ge(consts, 1)
            pool.affine_select(ident[:, :], ident[:, :], [[-1, P]], ALU.not_equal, 1.0, 0, 1)
            pool.affine_select(ident_bf[:, :], ident_bf[:, :], [[-1, P]], ALU.not_equal, 1.0, 0, 1)
            pool.affine_select(causal[:, (MT - 1) * P:], causal[:, (MT - 1) * P:], [[-1, P]], ALU.is_ge,
                               MASKED, 0, 1).then_inc(consts, 1)
            for b in range(2):
                pool.memset(v_st[b][:, :, :, D:], 0.0)
            pool.memset(max_bf[:, PARTS:, :], 0.0).then_inc(consts, 1)
            pool.wait_ge(consts, 3)
            pool.memset(v_st[0][:, :, :, D:D + 1], 1.0)
            pool.memset(v_st[1][:, :, :, D:D + 1], 1.0).then_inc(consts, 1)

            def inverse_root(chain, n, per):
                pool.wait_ge(chain, at(n, per, 3))
                pool.tensor_tensor(rstd[:, :], vareps[:, :], minus_half[:, :], ALU.pow).then_inc(chain, 1)

            def third_parts(n):
                for r in range(4):
                    pool.wait_ge(part2, at(n, 4, r + 1))
                    pool.tensor_tensor(part_sb[r][:, 2, :], rest_sb[r][:, :], part_sb[r][:, 1, :],
                                       ALU.subtract).then_inc(part3, 1)

            inverse_root(ln_a, 0, 4)
            inverse_root(ln_a, 1, 4)
            third_parts(0)
            with pool.Fori(0, NCH // 2 - 1) as i:
                for k in (1, 2):
                    inverse_root(ln_a, (i, k + 1), 4)
                    third_parts((i, k))
            third_parts(NCH - 1)
            pool.drain().then_inc(phase_a, 1)

            pool.wait_ge(phase_a, 4)
            for r in range(4):
                pool.wait_ge(stored[r], 16 * (NCH + 1))
            for b in range(2):
                pool.memset(k_st[b][ROWS:ROWS + PARTS, :, :], 1.0).then_inc(consts, 1)
                pool.wait_ge(consts, 5 + b)

            def stage_values(n, hg, b):
                v = v_all[:, b * QC:(b + 1) * QC, :, :].rearrange("p q t c -> p (q t) c")
                v = v[:, :, bass.ds(hg * GC, GC)].rearrange("p k (g e) -> p k g e", g=G)
                pool.tensor_copy(v_st[b][:, :, :, 0:D], v).then_inc(vst_ready, 1)

            def slot(n, key, hg):
                staged = key[1]
                for e in att[key]:
                    if e[0] != "scores":
                        continue
                    _, s, c, j, g = e
                    if j < TC * c or g % 2 == 0:
                        continue
                    off = (j - TC * c) * P
                    pool.wait_ge(exp_done, at(n, G * NS, G * s + g + 1 + SB))
                    pool.sem_inc(pool_passed, 1)
                    pr = probs[:, s % PB, g - 1:g + 1, off:off + P]
                    pool.affine_select(pr, pr, [[0, 2], [1, P]], ALU.is_ge, 0.0, 0, -1).then_inc(masked, 1)
                    if s == TC - 1 and g == G - 1 and not staged:
                        if n != 0:
                            pool.wait_ge(pv_done, at(n, NS, PB))
                        stage_values(nxt(n), hg, parity(nxt(n)))

            stage_values(0, 0, 0)
            slot(0, (False, False), 0)
            with pool.Fori(0, NG // 2 - 1) as i:
                slot((i, 1), (True, False), i + 1)
                slot((i, 2), (True, False), i + 1)
            slot(NG - 1, (True, True), 0)
            pool.drain().then_inc(phase_b, 1)
            pool.wait_ge(phase_b, 4)

            def split_w2(tiles):
                for k in tiles:
                    pool.wait_ge(w_hi, KC + k + 1)
                    pool.tensor_tensor(w2_lo[:, k, :], w2_sb[:, k, :], w2_hi[:, k, :].bitcast(F32),
                                       ALU.subtract).then_inc(w2_low, 1)

            inverse_root(ln_y, 0, 5)
            inverse_root(ln_x, 0, 4)
            split_w2(range(2))
            inverse_root(ln_y, 1, 5)
            split_w2(range(2, 4))
            inverse_root(ln_x, 1, 4)
            split_w2(range(4, SM))

            def roots(n, context):
                if context:
                    inverse_root(ln_y, nxt(n, 2), 5)
                inverse_root(ln_f, n, 5)
                if context:
                    inverse_root(ln_x, nxt(n, 2), 4)

            roots(0, True)
            with pool.Fori(0, NCH // 2 - 2) as i:
                roots((i, 1), True)
                roots((i, 2), True)
            roots(NCH - 3, True)
            roots(NCH - 2, False)
            roots(NCH - 1, False)

        @block.scalar
        def _(act):
            act.sem_inc(v_copied, 2)
            act.sem_inc(exp_done, SB)
            act.sem_inc(ctx_copied, 1)
            act.sem_inc(gelu_done, 2)

            def high_xt(n):
                for k in range(KC):
                    act.wait_ge(xt_ready, at(n, 2, k + 5))
                    nc.scalar.copy(xt_hi[parity(n)][:, k, :], xt_ps[k][:, :]).then_inc(xt_high, 1)

            def copy_v(n):
                for v in range(2):
                    act.wait_ge(v_ready, at(n, 2, v + 1))
                    dst = v_all[:, one(n), 2 * v:2 * v + 2, :].rearrange("p o t c -> p (o t c)")
                    nc.scalar.copy(dst, v_ps[v]).then_inc(v_copied, 1)

            def parts_12(n, turn_next):
                def first(r):
                    act.wait_ge(qk_ready, at(n, 4, r + 1))
                    act.wait_ge(stored[r], at(n, 16, 16))
                    nc.scalar.copy(part_sb[r][:, 0, :], qk_ps[r]).then_inc(part1, 1)

                def second(r):
                    act.wait_ge(rest1, at(n, 4, r + 5))
                    nc.scalar.copy(part_sb[r][:, 1, :], rest_sb[r][:, :]).then_inc(part2, 1)

                first(0)
                for r in range(1, 4):
                    first(r)
                    second(r - 1)
                if turn_next:
                    high_xt(nxt(n))
                second(3)

            act.wait_ge(qkv_in, 16 * 3)
            for w, hi in zip(wqkv_sb, wqkv_hi):
                nc.scalar.copy(hi[:, :, :], w[:, :, :]).then_inc(qkv_hi, 1)
            high_xt(0)
            parts_12(0, True)
            with act.Fori(0, NCH // 2 - 1) as i:
                for k in (1, 2):
                    copy_v((i, k - 1))
                    parts_12((i, k), True)
            copy_v(NCH - 2)
            parts_12(NCH - 1, False)
            copy_v(NCH - 1)
            act.drain().then_inc(phase_a, 1)
            act.wait_ge(phase_a, 4)

            def copy_context(c):
                nc.scalar.copy(ctx_sb[c % 2][:, :], ctx_ps[:, :]).then_inc(ctx_copied, 1)

            def slot(n, key):
                for e in att[key]:
                    if e[0] == "scores":
                        _, s, c, j, g = e
                        off = max(0, j - TC * c) * P
                        act.wait_ge(sc_ready, at(n, G * NS, G * s + g + 1))
                        if g == 0:
                            act.wait_ge(pv_done, at(n, NS, s + 1))
                        nc.scalar.activation(probs[:, s % PB, g, off:], score_ps[(G * s + g) % SB][:, off:], ACT.Exp,
                                             scale=1.0 / float(D) ** 0.5).then_inc(exp_done, 1)
                    elif e[0] == "context":
                        _, s, c, j = e
                        if j == TC * (c + 1) - 1:
                            act.wait_ge(pv_done, at(n, NS, s + 1 + PB))
                            copy_context(c)

            slot(0, (False, False))
            with act.Fori(0, NG // 2 - 1) as i:
                slot((i, 1), (True, False))
                slot((i, 2), (True, False))
            slot(NG - 1, (True, True))
            act.wait_ge(pv_done, NS * NG + PB)
            copy_context(QC - 1)
            act.drain().then_inc(phase_b, 1)
            act.wait_ge(phase_b, 4)
            act.wait_ge(w_in, 16 * N_WEIGHTS)

            def copy_context_turned(n):
                for k in range(KC):
                    act.wait_ge(ct_ready, at(n, 2, k + 1))
                    act.wait_ge(y_ready, at(n, 2, 2))
                    nc.scalar.copy(ct_sb[:, k, :], xt_ps[k][:, :]).then_inc(ct_copied, 1)

            def split_x1(n):
                for k in range(KC):
                    act.wait_ge(x1t_ready, at(n, 2, k + 3))
                    nc.scalar.copy(x1t_hi[:, k, :], xt_ps[k][:, :]).then_inc(x1t_high, 1)

            def gelu(n, m):
                if m == 0:
                    act.wait_ge(f_ready, at(n, 2, 2))
                act.wait_ge(h_ready, at(n, SM, m + 1))
                act.wait_ge(gelu_low, at(n, SM, m + 1))
                nc.scalar.activation(gelu_sb[m % GB], h_ps[m % 2], ACT.Gelu, bias=b1_sb[:, m:m + 1])
                nc.scalar.activation(ht_hi[:, m, :], h_ps[m % 2], ACT.Gelu,
                                     bias=b1_sb[:, m:m + 1]).then_inc(gelu_done, 1)

            copy_context_turned(0)
            for w, hi, tiles in ((w1_sb, w1_hi, KC), (w2_sb, w2_hi, SM)):
                for k in range(tiles):
                    nc.scalar.copy(hi[:, k, :], w[:, k, :]).then_inc(w_hi, 1)
                if w is w1_sb:
                    copy_context_turned(1)
            split_x1(0)

            def chunk(n, context, x1):
                for m in range(SM):
                    if context and m == SM - 2:
                        copy_context_turned(nxt(n, 2))
                    gelu(n, m)
                if x1:
                    split_x1(nxt(n))

            with act.Fori(0, NCH // 2 - 1) as i:
                chunk((i, 0), True, True)
                chunk((i, 1), True, True)
            chunk(NCH - 2, False, True)
            chunk(NCH - 1, False, False)

        @block.vector
        def _(dve):
            dve.sem_inc(rest1, 4)
            dve.sem_inc(xt_low, 2)
            dve.sem_inc(ring_done, RING)
            dve.sem_inc(y_taken, 2)
            dve.sem_inc(x1t_low, 4)
            dve.sem_inc(gelu_low, GB)
            dve.sem_inc(f_taken, 2)

            def norm_stats(src, chain, kind):
                for t in range(TC):
                    last = nc.vector.bn_stats(stats_sb[:, kind, t, :], src[:, t, :])
                last.then_inc(chain, 1)

            def norm_var(chain, n, per, kind):
                dve.wait_ge(chain, at(n, per, 1))
                dve.sem_inc(dve_passed, 1)
                for t in range(TC):
                    last = nc.vector.bn_aggr(meanvar_sb[:, kind, t, :], stats_sb[:, kind, t, :])
                last.then_inc(chain, 1)
                dve.wait_ge(chain, at(n, per, 2))
                nc.vector.tensor_scalar(vareps[:, :], meanvar_sb[:, kind, :, 1], EPS, None,
                                        ALU.add).then_inc(chain, 1)

            def norm_scale(src, dst, chain, n, per, kind):
                dve.wait_ge(chain, at(n, per, 4))
                for t in range(TC):
                    last = nc.vector.tensor_scalar(dst[:, t, :], src[:, t, :], meanvar_sb[:, kind, t, 0:1],
                                                   rstd[:, t:t + 1], ALU.subtract, ALU.mult)
                return last

            def layer_norm(src, dst, chain, n, per, kind):
                norm_stats(src, chain, kind)
                norm_var(chain, n, per, kind)
                return norm_scale(src, dst, chain, n, per, kind)

            def stats_x(n):
                b = parity(n)
                dve.wait_ge(x_in[b], at(n, 8, 16 - 8 * b))
                norm_stats(x_sb[b], ln_a, b)

            def scale_x(n):
                b = parity(n)
                dve.wait_ge(xt_ready, at(n, 2, 2))
                norm_scale(x_sb[b][:, :, :], xn_sb[b][:, :, :], ln_a, n, 4, b).then_inc(xn_ready, 1)

            def rest(n, r):
                dve.wait_ge(part1, at(n, 4, r + 1))
                nc.vector.tensor_tensor(rest_sb[r][:, :], qk_ps[r], part_sb[r][:, 0, :],
                                        ALU.subtract).then_inc(rest1, 1)

            def low_xt(n):
                b = parity(n)
                for k in range(KC):
                    dve.wait_ge(xt_high, at(n, 2, k + 1))
                    nc.vector.tensor_tensor(xt_lo[b][:, k, :], xt_ps[k][:, :], xt_hi[b][:, k, :].bitcast(F32),
                                            ALU.subtract).then_inc(xt_low, 1)

            def rest_parts(n, norm_next):
                if norm_next:
                    stats_x(nxt(n))
                rest(n, 0)
                if norm_next:
                    norm_var(ln_a, nxt(n), 4, parity(nxt(n)))
                rest(n, 1)
                if norm_next:
                    scale_x(nxt(n))
                rest(n, 2)
                rest(n, 3)
                if norm_next:
                    low_xt(nxt(n))

            stats_x(0)
            norm_var(ln_a, 0, 4, 0)
            scale_x(0)
            for z, (w, hi, lo) in enumerate(zip(wqkv_sb, wqkv_hi, wqkv_lo)):
                dve.wait_ge(qkv_hi, z + 1)
                nc.vector.tensor_tensor(lo[:, :, :], w[:, :, :], hi[:, :, :].bitcast(F32),
                                        ALU.subtract).then_inc(qkv_lo, 1)
            low_xt(0)
            rest_parts(0, True)
            with dve.Fori(0, NCH // 2 - 1) as i:
                for k in (1, 2):
                    rest_parts((i, k), True)
            rest_parts(NCH - 1, False)
            dve.drain().then_inc(phase_a, 1)
            dve.wait_ge(phase_a, 4)

            def take_max(use, head, t, p):
                dve.wait_ge(ring_ready, at(use[0], NR, use[1] + 1))
                w = min(MT, t + 1 - MT * p) * P
                dst = max_parts[:, t // TC % 2, head * TC + t % TC, p:p + 1]
                src = ring_ps[use[2]][:, 0:w]
                if p == t // MT:
                    dve.sem_inc(dve_passed, 1)
                    nc.vector.tensor_tensor_reduce(max_junk[:, use[2], 0:w], src, causal[:, MT * P - w:], 1.0, MASKED,
                                                   ALU.add, ALU.max, dst).then_inc(ring_done, 1)
                else:
                    nc.vector.reduce_max(dst, src, AX_X).then_inc(ring_done, 1)

            def split_max(n, c, use):
                def passed(step):
                    return at(n, 5 * QC, 5 * c + step)

                dve.wait_ge(ring_done, at(use[0], NR, use[1] + 1 + RING))
                nc.vector.reduce_max(max_q[:, :], max_parts[:, c % 2, :, 0:c + 1], AX_X).then_inc(m_chain, 1)
                dve.wait_ge(m_chain, passed(1))
                nc.vector.tensor_scalar(max_bf[:, 0, :], max_q[:, :], -1.0, None, ALU.mult).then_inc(m_chain, 1)
                dve.wait_ge(m_chain, passed(2))
                nc.vector.scalar_tensor_tensor(max_rest[:, :], max_q[:, :], -1.0, max_bf[:, 0, :],
                                               ALU.mult, ALU.subtract).then_inc(m_chain, 1)
                dve.wait_ge(m_chain, passed(3))
                nc.vector.tensor_copy(max_bf[:, 1, :], max_rest[:, :]).then_inc(m_chain, 1)
                dve.wait_ge(m_chain, passed(4))
                nc.vector.tensor_tensor(max_bf[:, 2, :], max_rest[:, :], max_bf[:, 1, :],
                                        ALU.subtract).then_inc(m_chain, 1)

            def copy_max_rows(n, c, use):
                dve.wait_ge(ring_ready, at(use[0], NR, use[1] + 1))
                if n != 0 or c > 0:
                    dve.wait_ge(mrow_in, at(n, 48 * QC, 48 * c))
                nc.vector.tensor_copy(max_rows[:, :],
                                      ring_ps[use[2]][:, 0:P // 2].bitcast(BF16)).then_inc(ring_done, 1)

            def normalise_context(n, use, c, hg, b):
                turn = ring_ps[use[2]][:, 0:CHUNK].rearrange("p (t g e) -> p t g e", t=TC, g=G)
                dve.wait_ge(ring_ready, at(use[0], NR, use[1] + 1))
                nc.vector.reciprocal(rden[:, c % 2], turn[:, :, :, D]).then_inc(rden_done, 1)
                dve.wait_ge(rden_done, at(n, QC, c + 1))
                dst = v_all[:, b * QC + c, :, bass.ds(hg * GC, GC)].rearrange("p t (g e) -> p t g e", g=G)
                scale = rden[:, c % 2].unsqueeze(3).to_broadcast([P, TC, G, D])
                nc.vector.tensor_tensor(dst, turn[:, :, :, 0:D], scale, ALU.mult).then_inc(ring_done, 1)

            dve.wait_ge(consts, 3)

            def maxima(n, e, use, last_max):
                if e[0] == "max":
                    take_max(use, *e[2:])
                elif e[0] == "split":
                    split_max(nxt(n, e[1]), e[2], last_max)
                elif e[0] == "turn_max":
                    copy_max_rows(nxt(n, e[1]), e[2], use)
                return use if e[0] == "max" else last_max

            last_max = None
            for e, use in first_uses():
                last_max = maxima(0, e, use, last_max)

            def slot(n, key, hg, hg_before):
                last_max = None
                for e, use in ring_uses(n, key):
                    if e[0] in ("max", "split", "turn_max"):
                        last_max = maxima(n, e, use, last_max)
                    elif e[0] == "turn":
                        if e[1] < 0:
                            normalise_context(nxt(n, -1), use, QC - 1, hg_before, parity(nxt(n, -1)))
                        else:
                            normalise_context(n, use, e[1], hg, parity(n))

            slot(0, (False, False), 0, 0)
            with dve.Fori(0, NG // 2 - 1) as i:
                slot((i, 1), (True, False), i, i)
                slot((i, 2), (True, False), i + 1, i)
            slot(NG - 1, (True, True), NG // 2 - 1, NG // 2 - 1)
            normalise_context(NG - 1, LAST_USE, QC - 1, NG // 2 - 1, 1)
            dve.drain().then_inc(phase_b, 1)
            dve.wait_ge(phase_b, 4)
            dve.wait_ge(w_in, 16 * N_WEIGHTS)

            def add_bias(n, v, ready, taken, ps, dst, bias):
                dve.wait_ge(ready, at(n, 2, v + 3))
                nc.vector.tensor_tensor(dst[:, 2 * v:2 * v + 2, :], ps[v].rearrange("p (t c) -> p t c", t=2),
                                        bias[:, :, :], ALU.add).then_inc(taken, 1)

            def attention_stats(n):
                for v in range(2):
                    add_bias(n, v, y_ready, y_taken, y_ps, yb_sb, bo_sb)
                dve.wait_ge(y_taken, at(n, 2, 4))
                norm_stats(yb_sb, ln_y, 0)
                norm_var(ln_y, n, 5, 0)

            def attention_norm(n):
                norm_scale(yb_sb, yb_sb, ln_y, n, 5, 0).then_inc(ln_y, 1)

            def first_residual(n):
                b = parity(n)
                dve.wait_ge(ln_y, at(n, 5, 5))
                dve.wait_ge(res_in[b], at(n, 8, 16 - 8 * b))
                nc.vector.tensor_tensor(x1_sb[b], yb_sb, res_sb[b], ALU.add).then_inc(res_free, 1)
                dve.wait_ge(res_free, at(n, 1, 1))
                norm_stats(x1_sb[b], ln_x, 1)
                norm_var(ln_x, n, 4, 1)

            def x1_norm(n):
                dve.wait_ge(x1t_ready, at(n, 2, 2))
                norm_scale(x1_sb[parity(n)], x1n_sb, ln_x, n, 4, 1).then_inc(x1n_ready, 1)

            def split_x1(n):
                for k in range(KC):
                    dve.wait_ge(x1t_high, at(n, 2, k + 1))
                    nc.vector.tensor_tensor(x1t_lo[:, k, :], xt_ps[k][:, :], x1t_hi[:, k, :].bitcast(F32),
                                            ALU.subtract).then_inc(x1t_low, 1)

            def split_hidden(n, m):
                dve.wait_ge(gelu_done, at(n, SM, m + 3))
                nc.vector.tensor_tensor(ht_lo[:, m, :], gelu_sb[m % GB], ht_hi[:, m, :].bitcast(F32),
                                        ALU.subtract).then_inc(gelu_low, 1)

            def mlp_norm(n):
                norm_scale(fb_sb, fb_sb, ln_f, n, 5, 2).then_inc(ln_f, 1)

            def second_residual(n):
                b = parity(n)
                dve.wait_ge(ln_f, at(n, 5, 5))
                dve.wait_ge(out_done[b], at(n, 8, 16 - 8 * b))
                nc.vector.tensor_tensor(o_sb[b], fb_sb, x1_sb[b], ALU.add).then_inc(o_ready, 1)

            def fix_context(n):
                if n != 0:
                    dve.wait_ge(ct_ready, at(n, 2))
                nc.vector.tensor_copy(cb_sb, v_all[:, one(n)].rearrange("p o t c -> p (o t) c")).then_inc(cb_ready, 1)

            fix_context(0)
            fix_context(1)
            for k in range(KC):
                dve.wait_ge(w_hi, k + 1)
                nc.vector.tensor_tensor(w1_lo[:, k, :], w1_sb[:, k, :], w1_hi[:, k, :].bitcast(F32),
                                        ALU.subtract).then_inc(w1_low, 1)
            attention_stats(0)
            fix_context(2)
            attention_norm(0)
            first_residual(0)
            x1_norm(0)
            attention_stats(1)
            split_x1(0)
            attention_norm(1)
            first_residual(1)

            def chunk(n, before, context, x1, fix=True):
                split_hidden(n, 0)
                if before:
                    prev = nxt(n, -1)
                    add_bias(prev, 1, f_ready, f_taken, f_ps, fb_sb, b2_sb)
                    dve.wait_ge(f_taken, at(prev, 2, 4))
                    split_hidden(n, 1)
                    norm_stats(fb_sb, ln_f, 2)
                    split_hidden(n, 2)
                    norm_var(ln_f, prev, 5, 2)
                    split_hidden(n, 3)
                    split_hidden(n, 4)
                    mlp_norm(prev)
                    split_hidden(n, 5)
                    second_residual(prev)
                    split_hidden(n, 6)
                    split_hidden(n, 7)
                    dve.wait_ge(o_ready, at(prev, 1, 1))
                    if x1:
                        first_residual(nxt(n))
                else:
                    for m in range(1, SM):
                        split_hidden(n, m)
                if x1:
                    x1_norm(nxt(n))
                if context:
                    attention_stats(nxt(n, 2))
                    if fix:
                        fix_context(nxt(n, 3))
                add_bias(n, 0, f_ready, f_taken, f_ps, fb_sb, b2_sb)
                if context:
                    attention_norm(nxt(n, 2))
                if x1:
                    split_x1(nxt(n))

            chunk(0, False, True, True)
            with dve.Fori(0, NCH // 2 - 2) as i:
                chunk((i, 1), True, True, True)
                chunk((i, 2), True, True, True)
            chunk(NCH - 3, True, True, True, fix=False)
            chunk(NCH - 2, True, False, True)
            chunk(NCH - 1, True, False, False)
            add_bias(NCH - 1, 1, f_ready, f_taken, f_ps, fb_sb, b2_sb)
            dve.wait_ge(f_taken, 2 * NCH + 2)
            norm_stats(fb_sb, ln_f, 2)
            norm_var(ln_f, NCH - 1, 5, 2)
            mlp_norm(NCH - 1)
            second_residual(NCH - 1)

        @block.tensor
        def _(pe):
            pe.sem_inc(xt_ready, 4)
            pe.sem_inc(pv_done, PB)
            pe.sem_inc(x1t_ready, 2)
            pe.sem_inc(y_ready, 2)
            pe.sem_inc(f_ready, 2)
            pe.wait_ge(consts, 2)

            def exact(dst, a_hi, a_lo, b_hi, b_lo, first, last):
                nc.tensor.matmul(dst, a_hi, b_hi, start=first, stop=False)
                nc.tensor.matmul(dst, a_hi, b_lo, start=False, stop=False)
                return nc.tensor.matmul(dst, a_lo, b_hi, start=False, stop=last)

            def turn_x(n):
                pe.wait_ge(xn_ready, at(n, 1, 1))
                pe.wait_ge(xt_low, at(n, 2, 2))
                for k in range(KC):
                    for t in range(TC):
                        last = nc.tensor.transpose(xt_ps[k][:, t * P:(t + 1) * P],
                                                   xn_sb[parity(n)][:, t, k * P:(k + 1) * P], ident[:, :])
                    last.then_inc(xt_ready, 1)

            def project_v(n):
                b = parity(n)
                for v in range(2):
                    pe.wait_ge(v_copied, at(n, 2, v + 1))
                    for t in (2 * v, 2 * v + 1):
                        rows = slice(t * P, (t + 1) * P)
                        for k in range(KC):
                            last = exact(v_ps[v][:, (t % 2) * C:(t % 2 + 1) * C], xt_hi[b][:, k, rows],
                                         xt_lo[b][:, k, rows], wqkv_hi[2][:, k, :], wqkv_lo[2][:, k, :],
                                         k == 0, k == KC - 1)
                    last.then_inc(v_ready, 1)

            def project_qk(n):
                pe.wait_ge(xt_low, at(n, 2, 4))
                b = parity(n)
                for r in range(4):
                    cols = slice((r % 2) * P, (r % 2 + 1) * P)
                    pe.wait_ge(rest1, at(n, 4, r + 1))
                    for k in range(KC):
                        last = exact(qk_ps[r], wqkv_hi[r // 2][:, k, cols], wqkv_lo[r // 2][:, k, cols],
                                     xt_hi[b][:, k, :], xt_lo[b][:, k, :], k == 0, k == KC - 1)
                    last.then_inc(qk_ready, 1)

            turn_x(0)
            pe.wait_ge(qkv_lo, 3)
            project_qk(0)
            with pe.Fori(0, NCH // 2 - 1) as i:
                for k in (1, 2):
                    turn_x((i, k))
                    project_v((i, k - 1))
                    project_qk((i, k))
            turn_x(NCH - 1)
            project_v(NCH - 2)
            project_qk(NCH - 1)
            project_v(NCH - 1)
            pe.drain().then_inc(phase_a, 1)
            pe.wait_ge(phase_a, 4)

            def max_scores(n, use, head, t, p):
                b = parity(n)
                if t == 0:
                    pe.wait_ge(st_in[b][head], at(n, 72, 144 - 72 * b))
                pe.wait_ge(ring_done, at(use[0], NR, use[3]))
                w = min(MT, t + 1 - MT * p) * P
                for a in range(0, w, CHUNK):
                    z = min(w, a + CHUNK)
                    last = nc.tensor.matmul(ring_ps[use[2]][:, a:z], q_st[b][0:ROWS, t // TC, head, t % TC * P:(t % TC + 1) * P],
                                            k_st[b][0:ROWS, head, p * MT * P + a:p * MT * P + z],
                                            start=True, stop=True)
                last.then_inc(ring_ready, 1)

            def turn_max(n, c, use):
                pe.wait_ge(ring_done, at(use[0], NR, use[3]))
                pe.wait_ge(m_chain, at(n, 5 * QC, 5 * (c + 1)))
                nc.tensor.transpose(ring_ps[use[2]][:, 0:P // 2].bitcast(BF16),
                                    max_bf[:, :, :].rearrange("p s m -> p (s m)"), ident_bf[:, :]).then_inc(ring_ready, 1)

            def scores(n, s, c, j, g):
                b = parity(n)
                off = max(0, j - TC * c) * P
                if j == 0 and g == 0:
                    pe.wait_ge(mrow_in, at(n, 48 * QC, 48 * (c + 1)))
                u = G * s + g
                if u >= SB:
                    pe.wait_ge(exp_done, at(n, G * NS, u + 1))
                else:
                    pe.wait_ge(exp_done, at(n, G * NS, SB - (G * NS - 1 - u) % SB))
                nc.tensor.matmul(score_ps[u % SB][:, off:],
                                 k_st[b][0:ROWS + PARTS, g, j * P:(j + 1) * P],
                                 q_st[b][0:ROWS + PARTS, c, g, off:],
                                 start=True, stop=True).then_inc(sc_ready, 1)

            def context(n, s, c, j):
                off = max(0, j - TC * c) * P
                if s == 0:
                    pe.wait_ge(vst_ready, at(n, 1, 1))
                if j == 0:
                    pe.wait_ge(ctx_copied, at(n, QC, c + 1))
                pe.wait_ge(exp_done, at(n, G * NS, G * s + G + SB))
                if j >= TC * c:
                    pe.wait_ge(masked, at(n, 2 * ND, 2 * (TC * c + j - TC * c) + 2))
                for g in range(G):
                    last = nc.tensor.matmul(ctx_ps[g * VW:(g + 1) * VW, off:], v_st[parity(n)][:, j, g, :],
                                            probs[:, s % PB, g, off:], start=(j == 0), stop=(j == TC * (c + 1) - 1))
                last.then_inc(pv_done, 1)

            def turn_context(n, use, c):
                pe.wait_ge(ctx_copied, at(n, QC, c + 2))
                pe.wait_ge(ring_done, at(use[0], NR, use[3]))
                for t in range(TC):
                    last = nc.tensor.transpose(ring_ps[use[2]][:, t * P:(t + 1) * P],
                                               ctx_sb[c % 2][:, t * P:(t + 1) * P], ident[:, :])
                last.then_inc(ring_ready, 1)

            def slot(n, key):
                for e, use in ring_uses(n, key):
                    if e[0] == "max":
                        max_scores(nxt(n, e[1]), use, *e[2:])
                    elif e[0] == "turn_max":
                        turn_max(nxt(n, e[1]), e[2], use)
                    elif e[0] == "turn":
                        if e[1] < 0:
                            turn_context(nxt(n, -1), use, QC - 1)
                        else:
                            turn_context(n, use, e[1])
                    elif e[0] == "scores":
                        scores(n, *e[1:])
                    elif e[0] == "context":
                        if e[1] < 0:
                            context(nxt(n, -1), NS + e[1], *e[2:])
                        else:
                            context(n, *e[1:])

            for e, use in first_uses():
                if e[0] == "max":
                    max_scores(0, use, *e[2:])
                elif e[0] == "turn_max":
                    turn_max(0, e[2], use)
            pe.wait_ge(consts, 6)
            slot(0, (False, False))
            with pe.Fori(0, NG // 2 - 1) as i:
                slot((i, 1), (True, False))
                slot((i, 2), (True, False))
            slot(NG - 1, (True, True))
            for s in range(NS - LAG, NS):
                context(NG - 1, s, *steps[s])
            turn_context(NG - 1, LAST_USE, QC - 1)
            pe.drain().then_inc(phase_b, 1)
            pe.wait_ge(phase_b, 4)
            pe.wait_ge(w_in, 16 * N_WEIGHTS)

            def turn_rows(src, ready):
                for k in range(KC):
                    for t in range(TC):
                        last = nc.tensor.transpose(xt_ps[k][:, t * P:(t + 1) * P], src[:, t, k * P:(k + 1) * P],
                                                   ident[:, :])
                    last.then_inc(ready, 1)

            def turn_context_rows(n):
                pe.wait_ge(cb_ready, at(n, 1, 1))
                if n == 1:
                    pe.wait_ge(ct_copied, 2)
                elif n != 0:
                    pe.wait_ge(x1t_low, at(n, 2, 2))
                turn_rows(cb_sb, ct_ready)

            def attention_out(n):
                pe.wait_ge(ct_copied, at(n, 2, 2))
                for v in range(2):
                    pe.wait_ge(y_taken, at(n, 2, v + 1))
                    for t in (2 * v, 2 * v + 1):
                        for k in range(KC):
                            last = nc.tensor.matmul(y_ps[v][:, (t % 2) * C:(t % 2 + 1) * C],
                                                    ct_sb[:, k, t * P:(t + 1) * P], wo_sb[:, k, :],
                                                    start=(k == 0), stop=(k == KC - 1))
                    last.then_inc(y_ready, 1)

            def turn_x1(n, ct_turned=1):
                pe.wait_ge(x1n_ready, at(n, 1, 1))
                pe.wait_ge(ct_copied, at(n, 2, 2 + 2 * ct_turned))
                turn_rows(x1n_sb, x1t_ready)

            def mlp_hidden(n, m):
                if m == 0:
                    pe.wait_ge(x1t_low, at(n, 2, 6))
                pe.wait_ge(gelu_done, at(n, SM, m + 1))
                cols = slice(m * P, (m + 1) * P)
                for k in range(KC):
                    last = exact(h_ps[m % 2], w1_hi[:, k, cols], w1_lo[:, k, cols], x1t_hi[:, k, :], x1t_lo[:, k, :],
                                 k == 0, k == KC - 1)
                last.then_inc(h_ready, 1)

            def mlp_output(n, v):
                pe.wait_ge(f_taken, at(n, 2, v + 1))
                for t in (2 * v, 2 * v + 1):
                    rows = slice(t * P, (t + 1) * P)
                    for m in range(SM):
                        if t == 0:
                            pe.wait_ge(gelu_low, at(n, SM, m + 1 + GB))
                        last = exact(f_ps[v][:, (t % 2) * C:(t % 2 + 1) * C], ht_hi[:, m, rows], ht_lo[:, m, rows],
                                     w2_hi[:, m, :], w2_lo[:, m, :], m == 0, m == SM - 1)
                last.then_inc(f_ready, 1)

            turn_context_rows(0)
            attention_out(0)
            turn_context_rows(1)
            attention_out(1)
            turn_x1(0)
            pe.wait_ge(w1_low, KC)

            def chunk(n, context, x1):
                for m in range(SM):
                    if context and m == SM - 2:
                        turn_context_rows(nxt(n, 2))
                    mlp_hidden(n, m)
                if context:
                    attention_out(nxt(n, 2))
                if n == 0:
                    pe.wait_ge(w2_low, SM)
                mlp_output(n, 0)
                if x1:
                    turn_x1(nxt(n), int(context))
                mlp_output(n, 1)

            chunk(0, True, True)
            with pe.Fori(0, NCH // 2 - 2) as i:
                chunk((i, 1), True, True)
                chunk((i, 2), True, True)
            chunk(NCH - 3, True, True)
            chunk(NCH - 2, False, True)
            chunk(NCH - 1, False, False)


_INS = ['L0_attn_x', 'L0_attn_W_q', 'L0_attn_W_k', 'L0_attn_W_v', 'L0_attn_W_o', 'L0_attn_b_o',
        'L0_ffn_w1', 'L0_ffn_b1', 'L0_ffn_w2', 'L0_ffn_b2']
_OUTS = [((2, 2048, 256), 'float32')]


def kernel(**inputs):
    import numpy as _np
    import concourse.bacc as _bacc
    from concourse import mybir as _mybir
    from concourse.bass_utils import run_bass_kernel_spmd as _run

    nc = _bacc.Bacc("TRN2", target_bir_lowering=False, num_devices=1)
    arrays, args = {}, []
    for name in _INS:
        a = _np.ascontiguousarray(inputs[name])
        arrays[f"in_{name}_dram"] = a
        args.append(nc.dram_tensor(f"in_{name}_dram", a.shape, _mybir.dt.from_np(a.dtype), kind="ExternalInput").ap())
    for i, (shape, dtype) in enumerate(_OUTS):
        dt = _mybir.dt.from_np(_np.dtype(dtype))
        args.append(nc.dram_tensor(f"out_{i}_dram", shape, dt, kind="ExternalOutput").ap())
    sandwich_kernel(nc, *args)
    r = _run(nc, [arrays], core_ids=[0])
    return r.results[0]["out_0_dram"]
```
